# Optimizing a Trainium2 kernel written in Bass

```python
import numpy as np
import jax
import jax.numpy as jnp

def _softmax(x, axis=-1):
    return jax.nn.softmax(x, axis=axis)

def _gelu(x):
    return jax.nn.gelu(x, approximate=True)

def _silu(x):
    return jax.nn.silu(x)

def _sigmoid(x):
    return jax.nn.sigmoid(x)

def _layernorm(x, axis=-1, eps=1e-05):
    m = jnp.mean(x, axis=axis, keepdims=True)
    v = jnp.var(x, axis=axis, keepdims=True)
    return (x - m) / jnp.sqrt(v + eps)

def _scatter_add(tgt, idx, src, axis=0):
    return tgt.at[idx].add(src)

def _segment_sum(src, seg, n):
    return jax.ops.segment_sum(src, seg, n)
kernel_name = 'mk_seq_preln_d1_jaxref_r8_bb5e73'

def setup_inputs(seed: int=0):
    np.random.seed(seed)
    _w = jnp.asarray

    def _L0_attn_setup():
        import jax, jax.numpy as jnp
        import numpy as np
        B, S, D, H = (4, 1024, 128, 16)
        DH = D // H
        key = jax.random.key(seed)
        ks = jax.random.split(key, 11)
        sc = 0.02
        return {'x': jax.random.normal(ks[0], (B, S, D), dtype=jnp.float32), 'Wp': jax.random.normal(ks[1], (D, D), dtype=jnp.float32) * sc, 'bp': jnp.zeros((D,), dtype=jnp.float32), 'Wq': jax.random.normal(ks[2], (D, D), dtype=jnp.float32) * sc, 'bq': jnp.zeros((D,), dtype=jnp.float32), 'Wk': jax.random.normal(ks[3], (D, D), dtype=jnp.float32) * sc, 'bk': jnp.zeros((D,), dtype=jnp.float32), 'Wv': jax.random.normal(ks[4], (D, D), dtype=jnp.float32) * sc, 'bv': jnp.zeros((D,), dtype=jnp.float32), 'Wo': jax.random.normal(ks[5], (D, D), dtype=jnp.float32) * sc, 'bo': jnp.zeros((D,), dtype=jnp.float32)}
    _L0_attn_in = _L0_attn_setup()

    def _L0_ffn_setup():
        import jax, jax.numpy as jnp
        import numpy as np
        D_MODEL = 128
        D_FF = 512
        N_EXPERTS = 8
        TOP_K = 2

        def _ffn(x, w1, b1, w2, b2):
            h = jax.nn.gelu(x @ w1.T + b1)
            return h @ w2.T + b2
        key = jax.random.key(seed)
        ks = jax.random.split(key, 12)
        s = 0.02
        x = jax.random.normal(ks[0], (4, 256, D_MODEL), dtype=jnp.float32)
        shared_w1 = jax.random.normal(ks[1], (D_FF, D_MODEL), dtype=jnp.float32) * s
        shared_b1 = jnp.zeros((D_FF,), dtype=jnp.float32)
        shared_w2 = jax.random.normal(ks[2], (D_MODEL, D_FF), dtype=jnp.float32) * s
        shared_b2 = jnp.zeros((D_MODEL,), dtype=jnp.float32)
        router_w = jax.random.normal(ks[3], (N_EXPERTS, D_MODEL), dtype=jnp.float32) * s
        router_b = jnp.zeros((N_EXPERTS,), dtype=jnp.float32)
        spec_w1 = jax.random.normal(ks[4], (N_EXPERTS, D_FF, D_MODEL), dtype=jnp.float32) * s
        spec_b1 = jnp.zeros((N_EXPERTS, D_FF), dtype=jnp.float32)
        spec_w2 = jax.random.normal(ks[5], (N_EXPERTS, D_MODEL, D_FF), dtype=jnp.float32) * s
        spec_b2 = jnp.zeros((N_EXPERTS, D_MODEL), dtype=jnp.float32)
        return dict(x=x, shared_w1=shared_w1, shared_b1=shared_b1, shared_w2=shared_w2, shared_b2=shared_b2, router_w=router_w, router_b=router_b, spec_w1=spec_w1, spec_b1=spec_b1, spec_w2=spec_w2, spec_b2=spec_b2)
    _L0_ffn_in = _L0_ffn_setup()
    _d = {'L0_attn_x': _L0_attn_in['x'], 'L0_attn_Wp': _L0_attn_in['Wp'], 'L0_attn_bp': _L0_attn_in['bp'], 'L0_attn_Wq': _L0_attn_in['Wq'], 'L0_attn_bq': _L0_attn_in['bq'], 'L0_attn_Wk': _L0_attn_in['Wk'], 'L0_attn_bk': _L0_attn_in['bk'], 'L0_attn_Wv': _L0_attn_in['Wv'], 'L0_attn_bv': _L0_attn_in['bv'], 'L0_attn_Wo': _L0_attn_in['Wo'], 'L0_attn_bo': _L0_attn_in['bo'], 'L0_ffn_shared_w1': _L0_ffn_in['shared_w1'], 'L0_ffn_shared_b1': _L0_ffn_in['shared_b1'], 'L0_ffn_shared_w2': _L0_ffn_in['shared_w2'], 'L0_ffn_shared_b2': _L0_ffn_in['shared_b2'], 'L0_ffn_router_w': _L0_ffn_in['router_w'], 'L0_ffn_router_b': _L0_ffn_in['router_b'], 'L0_ffn_spec_w1': _L0_ffn_in['spec_w1'], 'L0_ffn_spec_b1': _L0_ffn_in['spec_b1'], 'L0_ffn_spec_w2': _L0_ffn_in['spec_w2'], 'L0_ffn_spec_b2': _L0_ffn_in['spec_b2']}
    _x0 = _d['L0_attn_x']
    _d['L0_attn_x'] = jax.random.normal(jax.random.fold_in(jax.random.key(seed), 1), (4, 1024, 128), dtype=_x0.dtype)
    del _x0
    return _d

def reference(L0_attn_x, L0_attn_Wp, L0_attn_bp, L0_attn_Wq, L0_attn_bq, L0_attn_Wk, L0_attn_bk, L0_attn_Wv, L0_attn_bv, L0_attn_Wo, L0_attn_bo, L0_ffn_shared_w1, L0_ffn_shared_b1, L0_ffn_shared_w2, L0_ffn_shared_b2, L0_ffn_router_w, L0_ffn_router_b, L0_ffn_spec_w1, L0_ffn_spec_b1, L0_ffn_spec_w2, L0_ffn_spec_b2):

    def _L0_attn_ref(x, Wp, bp, Wq, bq, Wk, bk, Wv, bv, Wo, bo):
        import jax, jax.numpy as jnp
        import numpy as np
        B, S, D, H = (4, 1024, 128, 16)
        DH = D // H
        b, s, d = x.shape
        scale = 1.0 / jnp.sqrt(jnp.asarray(DH, dtype=x.dtype))
        xp = x @ Wp.T + bp
        q = ((xp @ Wq.T + bq) * scale).reshape(b, s, H, DH)
        k = (xp @ Wk.T + bk).reshape(b, s, H, DH)
        v = (xp @ Wv.T + bv).reshape(b, s, H, DH)
        i = jnp.arange(s)
        idx = jnp.stack([(i - 1) % s, i, (i + 1) % s], axis=1)
        kn = k[:, idx]
        vn = v[:, idx]
        scores = jnp.einsum('bshd,bsnhd->bshn', q, kn)
        attn = jax.nn.softmax(scores, axis=-1)
        out = jnp.einsum('bshn,bsnhd->bshd', attn, vn).reshape(b, s, d)
        return out @ Wo.T + bo

    def _L0_ffn_ref(x, shared_w1, shared_b1, shared_w2, shared_b2, router_w, router_b, spec_w1, spec_b1, spec_w2, spec_b2):
        import jax, jax.numpy as jnp
        import numpy as np
        D_MODEL = 128
        D_FF = 512
        N_EXPERTS = 8
        TOP_K = 2

        def _ffn(x, w1, b1, w2, b2):
            h = jax.nn.gelu(x @ w1.T + b1)
            return h @ w2.T + b2
        B, T, D = x.shape
        xf = x.reshape(-1, D)
        U = xf.shape[0]
        logits = xf @ router_w.T + router_b
        routing = jax.nn.softmax(logits, axis=-1)
        sel_w, sel_idx = jax.lax.top_k(routing, TOP_K)
        sel_w = sel_w / sel_w.sum(axis=-1, keepdims=True)
        comb = jnp.zeros_like(routing).at[jnp.arange(U)[:, None], sel_idx].set(sel_w)
        shared_out = _ffn(xf, shared_w1, shared_b1, shared_w2, shared_b2)

        def body(acc, params):
            w1, b1, w2, b2, we = params
            return (acc + we[:, None] * _ffn(xf, w1, b1, w2, b2), None)
        acc0 = jnp.zeros_like(shared_out)
        acc, _ = jax.lax.scan(body, acc0, (spec_w1, spec_b1, spec_w2, spec_b2, comb.T))
        return (shared_out + acc).reshape(B, T, D)
    x = L0_attn_x
    x = x + _L0_attn_ref(_layernorm(x, axis=-1), L0_attn_Wp, L0_attn_bp, L0_attn_Wq, L0_attn_bq, L0_attn_Wk, L0_attn_bk, L0_attn_Wv, L0_attn_bv, L0_attn_Wo, L0_attn_bo)
    x = x + _L0_ffn_ref(_layernorm(x, axis=-1), L0_ffn_shared_w1, L0_ffn_shared_b1, L0_ffn_shared_w2, L0_ffn_shared_b2, L0_ffn_router_w, L0_ffn_router_b, L0_ffn_spec_w1, L0_ffn_spec_b1, L0_ffn_spec_w2, L0_ffn_spec_b2)
    return x

_drawn_inputs = setup_inputs


def setup_inputs(seed=0):
    import zlib

    import numpy as np

    out = dict(_drawn_inputs(seed))
    spreads = {'L0_attn_bp': (0.0, 0.8),
     'L0_attn_bq': (0.0, 0.8),
     'L0_attn_bk': (0.0, 0.8),
     'L0_attn_bv': (0.0, 0.322),
     'L0_attn_bo': (0.0, 0.1),
     'L0_ffn_shared_b1': (0.0, 0.348),
     'L0_ffn_shared_b2': (0.0, 0.1),
     'L0_ffn_router_b': (0.0, 0.1),
     'L0_ffn_spec_b1': (0.0, 0.454),
     'L0_ffn_spec_b2': (0.0, 0.1)}
    factors = {'L0_attn_Wp': 6.236, 'L0_attn_Wq': 8.0, 'L0_attn_Wk': 8.0, 'L0_attn_Wv': 5.179}
    for name, (base, spread) in spreads.items():
        noise = np.random.default_rng([zlib.crc32(name.encode()), seed]).standard_normal(out[name].shape)
        drawn = base * np.exp(spread * noise) if base else spread * noise
        out[name] = jnp.asarray(drawn.astype(out[name].dtype))
    for name, factor in factors.items():
        out[name] = (out[name] * factor).astype(out[name].dtype)
    return out
```

```python
import concourse.bass as bass
from concourse import mybir
from contextlib import ExitStack

P = 128
BATCHES, SEQ, D = 4, 1024, 128
TOKENS = BATCHES * SEQ
HEADS = 16
HEAD_DIM = D // HEADS
NEIGH = 3
FF = 512
FC = FF // P
EXPERTS = 8
EPS = 1e-5

TB = SEQ // P
TILES = TOKENS // P
GROUPS = P // HEADS
GT = SEQ // GROUPS

SLOT = 256
SJ = SLOT // P
REGION = TOKENS + SLOT
PAD_ROW = EXPERTS * REGION
XG_ROWS = PAD_ROW + SLOT
ROW = D + 2
SLOT_TILES = 2 * TOKENS // SLOT + EXPERTS - 1
PAD_TOKEN = 4 * TOKENS
SH_TILES = TOKENS // SLOT


def preln_local_attention_moe(nc, x, wp, bp, wqkv_t, bqkv, wo_t, bo, sw1_t, sb1, sw2_t, sb2, rw_t, rb,
                              ew1_t, ew2_t, eb, out):
    fp32, fp32r = mybir.dt.float32, mybir.dt.float32r
    bf16, int32 = mybir.dt.bfloat16, mybir.dt.int32
    ALU = mybir.AluOpType
    ACT = mybir.ActivationFunctionType
    X = mybir.AxisListType.X
    SCALE = float(HEAD_DIM) ** -0.5

    xg = nc.dram_tensor("rows_by_expert", (XG_ROWS, ROW), fp32, kind="Internal").ap()
    yg = nc.dram_tensor("expert_outputs", (2 * TOKENS, D), fp32, kind="Internal").ap()

    with ExitStack() as ctx:
        def sb(name, shape, dt=fp32):
            return ctx.enter_context(nc.sbuf_tensor(name, shape, dt))

        def sem(name):
            return ctx.enter_context(nc.semaphore(name))

        bank = [ctx.enter_context(nc.psum_tensor(f"bank{i}", [P, 512], fp32)) for i in range(8)]

        ident = sb("ident", [P, P])
        score_mask = sb("score_mask", [P, 2 * P - HEADS])
        expand = sb("expand", [P, GROUPS, P], fp32r)
        before = sb("before", [P, P], bf16)
        ones_bf = sb("ones_bf", [P, P], bf16)
        rank_weight = sb("rank_weight", [P, EXPERTS])
        region_start = sb("region_start", [P, EXPERTS])
        half_neg = sb("half_neg", [P, TB])
        slot_no = sb("slot_no", [P, SLOT_TILES])
        pad_rows = sb("pad_rows", [P, SJ, ROW])

        wp_sb = sb("wp_sb", [P, D])
        wqkv_sb = sb("wqkv_sb", [P, 3 * D])
        wcomb = sb("wcomb", [P, 3 * D])
        bp_sb = sb("bp_sb", [P, 1])
        bqkv_sb = sb("bqkv_sb", [P, 3])
        bcomb = sb("bcomb", [P, 3])
        wo_sb = sb("wo_sb", [P, D])
        bo_bc = sb("bo_bc", [P, D])
        rw_sb = sb("rw_sb", [P, EXPERTS])
        rw_hi = sb("rw_hi", [P, EXPERTS], fp32r)
        rw_lo = sb("rw_lo", [P, EXPERTS], fp32r)
        rb_bc = sb("rb_bc", [P, EXPERTS])

        x_all = sb("x_all", [P, TILES, D])
        rows = sb("rows", [P, TB, ROW])
        xt_hi = sb("xt_hi", [P, TOKENS], fp32r)
        xt_lo = sb("xt_lo", [P, TOKENS], fp32r)
        gate1 = sb("gate1", [P, TILES])
        gate2 = sb("gate2", [P, TILES])
        pos1 = sb("pos1", [P, TILES], int32)
        pos2 = sb("pos2", [P, TILES], int32)

        w_all = sb("w_all", [P, EXPERTS, 4, FF], fp32r)
        b_all = sb("b_all", [P, EXPERTS, FC + 1])
        b_stage = [sb(f"b_stage{i}", [P, FC + 1]) for i in range(2)]
        sb1_sb = sb("sb1_sb", [P, FC])
        sb2_sb = sb("sb2_sb", [P, 1])

        w_raw = sb("w_raw", [P, FF])
        sw = sb("sw", [P, 4, FF], fp32r)
        h_hi = [sb(f"h_hi{i}", [P, FC, SLOT], fp32r) for i in range(2)]
        h_lo = [sb(f"h_lo{i}", [P, FC, SLOT], fp32r) for i in range(2)]
        stage = [xt[:, 0:4 * FF].rearrange("p (w f) -> p w f", w=4) for xt in (xt_hi, xt_lo)]
        xs_hi = [xt[:, 4 * FF:4 * FF + SLOT] for xt in (xt_hi, xt_lo)]
        xs_lo = [xt[:, 4 * FF + SLOT:4 * FF + 2 * SLOT] for xt in (xt_hi, xt_lo)]

        ARENA = 3 * SEQ + 3 * (SEQ + 2) + NEIGH * SEQ
        arena = sb("arena", [P, ARENA])
        at = [0]

        def piece(n):
            at[0] += n
            assert at[0] <= ARENA
            return arena[:, at[0] - n:at[0]]

        xn = piece(TB * D).rearrange("p (t d) -> p t d", d=D)
        xnt = piece(SEQ)
        attn = xnt
        q_sb = piece(SEQ)
        k_sb = piece(SEQ + 2)
        v_sb = [piece(SEQ + 2) for _ in range(2)]
        prod = piece(NEIGH * SEQ).rearrange("p (n t) -> p n t", n=NEIGH)
        expand_raw = prod[:, 0, :]
        at[0] = 0
        h_sb = [piece(FC * SLOT).rearrange("p (c t) -> p c t", c=FC) for _ in range(2)]
        yt = [piece(SLOT) for _ in range(2)]
        y_sb = [piece(SLOT).rearrange("p (j d) -> p j d", j=SJ) for _ in range(2)]
        xs = [piece(SJ * ROW).rearrange("p (j d) -> p j d", j=SJ) for _ in range(2)]
        y_back = [piece(2 * 4 * D).rearrange("p (t kd) -> p t kd", t=4) for _ in range(2)]
        passed = piece(SLOT_TILES * EXPERTS).rearrange("p (s e) -> p s e", e=EXPERTS)
        passed_n = piece(SLOT_TILES * EXPERTS).rearrange("p (s e) -> p s e", e=EXPERTS)
        st = sb("st", [P, TB, 6])
        mv = sb("mv", [P, TB, 2])
        rstd = sb("rstd", [P, TB])
        st2 = sb("st2", [P, TB, 6])
        mv2 = sb("mv2", [P, TB, 2])
        rstd2 = sb("rstd2", [P, TB])
        top = sb("top", [P, GT])
        soft = sb("soft", [P, NEIGH, GT])
        p_hi = sb("p_hi", [P, NEIGH, GT], fp32r)
        p_lo = sb("p_lo", [P, NEIGH, GT], fp32r)
        inv = sb("inv", [P, GT])
        weighted = sb("weighted", [P, NEIGH, 512])

        lg = sb("lg", [P, TB, EXPERTS])
        cand = sb("cand", [P, TB, EXPERTS])
        sel1 = sb("sel1", [P, TB, EXPERTS])
        sel2 = sb("sel2", [P, TB, EXPERTS])
        either = sb("either", [P, TB, EXPERTS], bf16)
        m1 = sb("m1", [P, TB])
        m2 = sb("m2", [P, TB])
        km = sb("km", [P, TB])
        eg = sb("eg", [P, TB])
        gap = sb("gap", [P, TB])
        slot_at = sb("slot_at", [P, TB, EXPERTS])
        base = sb("base", [P, EXPERTS])

        n_int = sb("n_int", [P, EXPERTS], int32)
        n_tiles = sb("n_tiles", [P, EXPERTS])
        ends = sb("ends", [P, 4, 4 + EXPERTS])
        pad_at = sb("pad_at", [P, EXPERTS], int32)
        slot_expert = sb("slot_expert", [P, SLOT_TILES])
        n_passed = sb("n_passed", [P, SLOT_TILES])
        row_f = sb("row_f", [P, SLOT_TILES])
        slot_row = sb("slot_row", [P, SLOT_TILES], int32)
        slot_w = sb("slot_w", [P, SLOT_TILES], int32)
        y_rows = sb("y_rows", [P, SJ * SLOT_TILES], int32)
        y_row = [sb(f"y_row{i}", [P, SJ], int32) for i in range(2)]

        TIN, DOWN, TOUT = (4, 7), 5, 6
        W_LOADS = 16 * 8
        out_view = lambda g: out.rearrange("b s d -> (b s) d")[g * 4 * P:(g + 1) * 4 * P, :].rearrange(
            "(t p) d -> p t d", p=P)

        x_in = [sem(f"x_in{b}") for b in range(BATCHES)]
        w_in = sem("w_in")
        bias_in = sem("bias_in")
        raw_in = sem("raw_in")
        raw_hi = sem("raw_hi")
        raw_lo = sem("raw_lo")
        const_ready = sem("const_ready")
        pool_step, dve_step, act_step = sem("pool_step"), sem("dve_step"), sem("act_step")
        comb_ready = sem("comb_ready")
        comb_w = sem("comb_w")
        comb_b = sem("comb_b")
        stat1, norm1 = sem("stat1"), sem("norm1")
        bo_added = sem("bo_added")
        proj_ready = sem("proj_ready")
        proj_out = sem("proj_out")
        halo = sem("halo")
        prod_done = sem("prod_done")
        scores = sem("scores")
        shifted = sem("shifted")
        exps = sem("exps")
        probs, probs_hi, probs_lo = sem("probs"), sem("probs_hi"), sem("probs_lo")
        spread = sem("spread")
        weighted_v = sem("weighted_v")
        attn_done = sem("attn_done")
        y_ready = sem("y_ready")
        resid = sem("resid")
        stat2, norm2 = sem("stat2"), sem("norm2")
        t2_ready = sem("t2_ready")
        xt_hi_done, xt_lo_done = sem("xt_hi_done"), sem("xt_lo_done")
        rw_split = sem("rw_split")
        logits = sem("logits")
        chosen = sem("chosen")
        ranks = sem("ranks")
        gap_ready, gap_exp = sem("gap_ready"), sem("gap_exp")
        routed = sem("routed")
        scattered = sem("scattered")
        tables = sem("tables")
        pad_out = sem("pad_out")
        y_in = [sem(f"y_in{i}") for i in range(2)]
        summed = sem("summed")
        out_done = sem("out_done")

        class Phase:
            def __init__(self, name):
                self.rows_in = [sem(f"{name}_rows_in{i}") for i in range(2)]
                self.w_in = [sem(f"{name}_w_in{i}") for i in range(2)]
                self.tin = sem(f"{name}_tin")
                self.xs_hi = sem(f"{name}_xs_hi")
                self.xs_lo = sem(f"{name}_xs_lo")
                self.up = sem(f"{name}_up")
                self.gelu = sem(f"{name}_gelu")
                self.h_hi = sem(f"{name}_h_hi")
                self.h_lo = sem(f"{name}_h_lo")
                self.down = sem(f"{name}_down")
                self.yt = sem(f"{name}_yt")
                self.tout = sem(f"{name}_tout")
                self.y = sem(f"{name}_y")
                self.idx = sem(f"{name}_idx")
                self.row, self.go = sem(f"{name}_row"), sem(f"{name}_go")
                self.y_out = [sem(f"{name}_y_out{i}") for i in range(2)]

        sh, ex = Phase("sh"), Phase("ex")

        block = ctx.enter_context(nc.Block())

        def chain(eng, signal):
            n = [0]

            def link(ins):
                n[0] += 1
                ins.then_inc(signal, 1)
                eng.wait_ge(signal, n[0])
            return link

        def wait(eng, signal, value):
            if not isinstance(value, int) or value > 0:
                eng.wait_ge(signal, value)

        def steady(eng, first, last, step):
            assert first % 2 == 0 and (last - first) % 2 == 1
            with eng.Fori(0, (last - first + 1) // 2) as pair:
                for par in range(2):
                    step(eng, pair * 2 + (first + par), par, pair + first // 2)

        def pipeline(eng, tiles, ahead, behind, step):
            first, last = behind + behind % 2, tiles - 1 - ahead
            if (last - first) % 2 == 0:
                last -= 1
            for i in range(-ahead, first):
                step(eng, i, i % 2, i // 2)
            steady(eng, first, last, step)
            for i in range(last + 1, tiles + behind):
                step(eng, i, i % 2, i // 2)

        def runs(i, back, tiles):
            return not isinstance(i, int) or 0 <= i - back < tiles

        WEIGHT_PIECES = 2 * (EXPERTS + 1)

        def raw_piece(n):
            if n < 2:
                src, dst = (sw1_t, sw2_t)[n], sw
                e = None
            else:
                e = (n - 2) // 2
                src, dst = (ew1_t, ew2_t)[n % 2][e], w_all[:, e]
            dst = sw[:, :, :] if e is None else w_all[:, e, :, :]
            return src, dst[:, 2 * (n % 2), :], dst[:, 2 * (n % 2) + 1, :]

        @block.sync
        def _(sp):
            for b in range(BATCHES):
                sp.dma_start(x_all[:, b * TB:(b + 1) * TB, :],
                             x[b].rearrange("(t p) d -> p t d", p=P)).then_inc(x_in[b], 16)
            for n in range(WEIGHT_PIECES):
                wait(sp, raw_lo, n)
                src = raw_piece(n)[0]
                if n % 2:
                    sp.dma_start(w_raw[:, :].rearrange("p (c d) -> p c d", c=FC),
                                 src.rearrange("(c p) d -> p c d", p=P)).then_inc(raw_in, 16)
                else:
                    sp.dma_start(w_raw[:, :], src).then_inc(raw_in, 16)

            sp.wait_ge(tables, 1)
            for e in range(EXPERTS):
                row = sp.value_load(pad_at[0:1, e:e + 1], min_val=e * REGION, max_val=e * REGION + TOKENS)
                sp.dma_start(xg[bass.ds(row, SLOT), :].rearrange("(j p) c -> p j c", p=P),
                             pad_rows[:, :, :]).then_inc(pad_out, 16)
            sp.dma_start(xg[PAD_ROW:PAD_ROW + SLOT, :].rearrange("(j p) c -> p j c", p=P),
                         pad_rows[:, :, :]).then_inc(pad_out, 16)
            sp.wait_ge(pad_out, 16 * (EXPERTS + 1))
            sp.wait_ge(scattered, 16 * 2 * TILES)
            sp.wait_ge(sh.up, SH_TILES)
            sp.wait_ge(raw_lo, WEIGHT_PIECES)
            sp.wait_ge(raw_hi, WEIGHT_PIECES)

            def load_tile(sp, i, par, half):
                if not runs(i, -1, SLOT_TILES):
                    return
                i, par = i + 1, 1 - par
                half = half + (1 - par)
                row = sp.value_load(slot_row[0:1, bass.ds(i, 1)], min_val=0, max_val=PAD_ROW)
                e = sp.value_load(slot_w[0:1, bass.ds(i, 1)], min_val=0, max_val=EXPERTS - 1)
                wait(sp, ex.tin, i - 1)
                wait(sp, ex.idx, i - 1)
                sp.dma_start(xs[par], xg[bass.ds(row, SLOT), :].rearrange("(j p) c -> p j c", p=P))\
                    .then_inc(ex.rows_in[par], 16)
                wait(sp, ex.down, i - 1)
                wait(sp, ex.yt, i - 1)
                sp.dma_start(stage[par].bitcast(fp32),
                             w_all[:, bass.ds(e, 1), :, :].rearrange("p a w f -> p (a w) f").bitcast(fp32))\
                    .then_inc(ex.w_in[par], 16)
                sp.dma_start(b_stage[par][:, :], b_all[:, bass.ds(e, 1), :].rearrange("p a c -> p (a c)"))\
                    .then_inc(ex.w_in[par], 16)
            pipeline(sp, SLOT_TILES, 1, 0, load_tile)

            for par in range(2):
                sp.wait_ge(ex.y_out[par], 16 * SJ * ((SLOT_TILES + 1 - par) // 2))
            for g in range(TILES // 4):
                wait(sp, summed, g - 1)
                sp.dma_start(y_back[g % 2], yg[g * 8 * P:(g + 1) * 8 * P, :]
                             .rearrange("(t p k) d -> p t (k d)", p=P, k=2)).then_inc(y_in[g % 2], 16)
                if g >= 1:
                    sp.wait_ge(summed, g)
                    sp.dma_start(out_view(g - 1), x_all[:, (g - 1) * 4:g * 4, :]).then_inc(out_done, 16)
            sp.wait_ge(summed, TILES // 4)
            sp.dma_start(out_view(TILES // 4 - 1), x_all[:, TILES - 4:TILES, :]).then_inc(out_done, 16)
            sp.wait_ge(out_done, 16 * (TILES // 4))

        @block.gpsimd
        def _(pool):
            link = chain(pool, pool_step)
            g = nc.gpsimd
            link(g.memset(ident[:, :], 0.0))
            link(g.affine_select(out=ident[:, :], in_=ident[:, :], compare_op=ALU.not_equal, fill=1.0,
                                 base=0, pattern=[[-1, P]], channel_multiplier=1))
            link(g.memset(half_neg[:, :], -0.5))

            def norm(b, stats, stats_ready, r, src, dst, dst_done):
                pool.wait_ge(stats_ready, b + 1)
                link(g.tensor_scalar_add(r[:, :], stats[:, :, 1], EPS))
                link(g.tensor_tensor(r[:, :], r[:, :], half_neg[:, :], ALU.pow))
                for t in range(TB):
                    last = g.tensor_scalar(dst[:, t, 0:D], src[:, b * TB + t, :], stats[:, t, 0:1], r[:, t:t + 1],
                                           ALU.subtract, ALU.mult)
                last.then_inc(dst_done, 1)

            def norm1_batch(b):
                if b >= 1:
                    pool.wait_ge(proj_ready, 8 * (b - 1) + 2)
                norm(b, mv, stat1, rstd, x_all, xn, norm1)
                pool.wait_ge(norm1, b + 1)
                pool.wait_ge(w_in, W_LOADS)
                xb = x_all[:, b * TB:(b + 1) * TB, :]
                g.tensor_tensor(xb, xb, bo_bc[:, :].unsqueeze(1).to_broadcast([P, TB, D]), ALU.add)\
                    .then_inc(bo_added, 1)

            def weight_lo(n):
                _, hi, lo = raw_piece(n)
                pool.wait_ge(raw_hi, n + 1)
                g.tensor_tensor(lo, w_raw[:, :], hi.bitcast(fp32), ALU.subtract).then_inc(raw_lo, 1)

            norm1_batch(0)
            link(g.memset(score_mask[:, :], 1.0))
            link(g.affine_select(out=score_mask[:, :], in_=score_mask[:, :], compare_op=ALU.is_ge, fill=0.0,
                                 base=HEAD_DIM * (P - HEADS), pattern=[[-HEAD_DIM, 2 * P - HEADS]],
                                 channel_multiplier=1))
            link(g.affine_select(out=score_mask[:, :], in_=score_mask[:, :], compare_op=ALU.is_ge, fill=0.0,
                                 base=HEAD_DIM - 1 - HEAD_DIM * (P - HEADS),
                                 pattern=[[HEAD_DIM, 2 * P - HEADS]], channel_multiplier=-1))
            link(g.memset(expand_raw[:, :], 0.0))
            link(g.affine_select(out=expand_raw[:, :], in_=expand_raw[:, :], compare_op=ALU.not_equal,
                                 fill=1.0, base=0, pattern=[[-HEADS, GROUPS], [-1, HEADS], [0, HEAD_DIM]],
                                 channel_multiplier=1))
            link(g.tensor_copy(expand[:, :, :].rearrange("p g d -> p (g d)"), expand_raw[:, :]))
            link(g.memset(ones_bf[:, :], 1.0))
            link(g.affine_select(out=before[:, :], in_=ones_bf[:, :], compare_op=ALU.is_gt, fill=0.0,
                                 base=0, pattern=[[1, P]], channel_multiplier=-1))
            link(g.iota(rank_weight[:, :], pattern=[[-1, EXPERTS]], base=EXPERTS, channel_multiplier=0,
                        allow_small_or_imprecise_dtypes=True))
            link(g.iota(region_start[:, :], pattern=[[REGION, EXPERTS]], base=0, channel_multiplier=0,
                        allow_small_or_imprecise_dtypes=True))
            link(g.tensor_copy(base[:, :], region_start[:, :]))
            link(g.iota(slot_no[:, :], pattern=[[1, SLOT_TILES]], base=0, channel_multiplier=0,
                        allow_small_or_imprecise_dtypes=True))
            link(g.memset(ends[:, :, :], 0.0))
            link(g.memset(pad_rows[:, :, :], 0.0))
            link(g.memset(pad_rows[:, :, D:D + 1], float(PAD_TOKEN)))
            g.memset(pad_rows[:, :, D + 1:D + 2], -1.0).then_inc(const_ready, 1)

            pieces = iter(range(WEIGHT_PIECES))
            for b in range(BATCHES + 1):
                if b < BATCHES:
                    pool.wait_ge(proj_out, 8 * b + 8)
                    v = v_sb[b % 2]
                    for buf in (k_sb, v):
                        g.tensor_copy(buf[:, 0:1], buf[:, SEQ:SEQ + 1])
                        last = g.tensor_copy(buf[:, SEQ + 1:SEQ + 2], buf[:, 1:2])
                    last.then_inc(halo, 1)
                if b + 1 < BATCHES:
                    norm1_batch(b + 1)
                for _ in range(4):
                    n = next(pieces, None)
                    if n is not None:
                        weight_lo(n)
                if b >= 1:
                    c = b - 1
                    if c >= 1:
                        pool.wait_ge(scattered, 16 * 2 * TB * c)
                        pool.wait_ge(t2_ready, 2 * c)
                    norm(c, mv2, stat2, rstd2, x_all, rows, norm2)
                    link(g.iota(rows[:, :, D:D + 1], pattern=[[2 * P, TB], [0, 1]], base=2 * c * SEQ,
                                channel_multiplier=2, allow_small_or_imprecise_dtypes=True))
                    pool.wait_ge(norm2, c + 1)
                    pool.wait_ge(routed, c + 1)
                    for t in range(TB):
                        for pos in (pos1, pos2):
                            g.indirect_dma_start(
                                xg[:, :], bass.IndirectOffsetOnAxis(ap=pos[:, c * TB + t:c * TB + t + 1], axis=0),
                                rows[:, t, :], None).then_inc(scattered, 16)
            pool.wait_ge(tables, 1)

            last_row = pool.to_reg(2 * TOKENS - 1)

            def put_tile(pool, i, par, half):
                k = i - 2
                if runs(i, 2, SLOT_TILES):
                    wait(pool, ex.y_out[par], (half - 1) * 16 * SJ)
                    pool.wait_ge(ex.idx, k + 1)
                    g.tensor_copy(y_row[par][:, :], y_rows[:, bass.ds(k * SJ, SJ)]).then_inc(ex.row, 1)
                    pool.wait_ge(ex.row, k + 1)
                    pool.wait_ge(ex.y, k + 1)
                    pool.sem_inc(ex.go, 1)
                    for j in range(SJ):
                        g.indirect_dma_start(
                            yg[:, :], bass.IndirectOffsetOnAxis(ap=y_row[par][:, j:j + 1], axis=0),
                            y_sb[par][:, j, :], None, bounds_check=last_row, oob_is_err=False)\
                            .then_inc(ex.y_out[par], 16)
            pipeline(pool, SLOT_TILES, 0, 2, put_tile)

        @block.scalar
        def _(act):
            a = nc.scalar
            act.dma_start(wp_sb[:, :], wp).then_inc(w_in, 16)
            act.dma_start(wqkv_sb[:, :], wqkv_t).then_inc(w_in, 16)
            act.dma_start(bp_sb[:, :], bp.rearrange("(p a) -> p a", a=1)).then_inc(w_in, 16)
            act.dma_start(bqkv_sb[:, :], bqkv).then_inc(w_in, 16)
            act.dma_start(wo_sb[:, :], wo_t).then_inc(w_in, 16)
            act.dma_start(rw_sb[:, :], rw_t).then_inc(w_in, 16)
            act.dma_start(bo_bc[:, :], bo.rearrange("(a n) -> a n", a=1).to_broadcast([P, D])).then_inc(w_in, 16)
            act.dma_start(rb_bc[:, :], rb.rearrange("(a n) -> a n", a=1).to_broadcast([P, EXPERTS])).then_inc(w_in, 16)
            act.dma_start(sb1_sb[:, :], sb1).then_inc(bias_in, 16)
            act.dma_start(sb2_sb[:, :], sb2.rearrange("(p a) -> p a", a=1)).then_inc(bias_in, 16)
            act.dma_start(b_all[:, :, :], eb).then_inc(bias_in, 16)

            act.wait_ge(comb_ready, 1)
            a.activation(wcomb[:, :], bank[0][:, 0:3 * D], ACT.Copy).then_inc(comb_w, 1)

            def weight_hi(n):
                _, hi, _ = raw_piece(n)
                act.wait_ge(raw_in, 16 * (n + 1))
                a.activation(hi, w_raw[:, :], ACT.Copy).then_inc(raw_hi, 1)

            pieces = iter(range(WEIGHT_PIECES))
            use = 0
            for b in range(BATCHES + 1):
                if b >= 1:
                    c = b - 1
                    act.wait_ge(shifted, c + 1)
                    a.activation(soft[:, :, :], soft[:, :, :], ACT.Exp).then_inc(exps, 1)
                if b < BATCHES:
                    targets = [(xnt, None)] * 2 + [(q_sb, 0)] * 2 + [(k_sb[:, 1:], 1)] * 2 + [(v_sb[b % 2][:, 1:], 2)] * 2
                    for j, (dst, which) in enumerate(targets):
                        if j == 0:
                            wait(act, y_ready, 2 * (b - 1))
                        if j == 2:
                            wait(act, prod_done, NEIGH * b)
                        if j == 6:
                            wait(act, attn_done, 2 * (b - 1))
                        act.wait_ge(proj_ready, use + 1)
                        dst = dst[:, (j % 2) * 512:(j % 2 + 1) * 512]
                        if which is None:
                            a.activation(dst, bank[use % 2][:, :], ACT.Copy).then_inc(proj_out, 1)
                        else:
                            a.activation(dst, bank[use % 2][:, :], ACT.Identity, bias=bcomb[:, which:which + 1],
                                         scale=SCALE if which == 0 else 1.0).then_inc(proj_out, 1)
                        use += 1
                if b >= 1:
                    act.wait_ge(probs, c + 1)
                    wait(act, spread, 2 * NEIGH * c)
                    a.activation(p_hi[:, :, :], soft[:, :, :], ACT.Copy).then_inc(probs_hi, 1)
                for _ in range(4):
                    n = next(pieces, None)
                    if n is not None:
                        weight_hi(n)
                if b >= 1:
                    for j in range(2):
                        act.wait_ge(t2_ready, 2 * c + j + 1)
                        a.activation(xt_hi[:, c * SEQ + j * 512:c * SEQ + (j + 1) * 512], bank[5 + j][:, :],
                                     ACT.Copy).then_inc(xt_hi_done, 1)
                    act.wait_ge(gap_ready, c + 1)
                    a.activation(eg[:, :], gap[:, :], ACT.Exp).then_inc(gap_exp, 1)
            act.wait_ge(bias_in, 16 * 3)

            def ffn_act(act, i, par, half, ph, tiles, b1_of, b2_of):
                if ph is ex and runs(i, -1, tiles):
                    act.wait_ge(ph.tin, i + 2)
                    wait(act, ph.up, i)
                    a.activation(xs_hi[1 - par], bank[TIN[1 - par]][:, 0:SLOT], ACT.Copy).then_inc(ph.xs_hi, 1)
                if runs(i, 0, tiles):
                    act.wait_ge(ph.up, i + 1)
                    wait(act, ph.h_lo, i - 1)
                    if ph is ex:
                        act.wait_ge(ph.w_in[par], (half + 1) * 32)
                    for c in range(FC):
                        last = a.activation(h_sb[par][:, c, :], bank[2 * par + c // 2][:, (c % 2) * SLOT:(c % 2 + 1) * SLOT],
                                            ACT.Gelu_apprx_tanh, bias=b1_of(par)[:, c:c + 1])
                    last.then_inc(ph.gelu, 1)
                if runs(i, 1, tiles):
                    act.wait_ge(ph.down, i)
                    wait(act, ph.tout, i - 2)
                    a.activation(yt[1 - par], bank[DOWN][:, 0:SLOT], ACT.Identity, bias=b2_of(1 - par))\
                        .then_inc(ph.yt, 1)

            pipeline(act, SH_TILES, 0, 2, lambda act, i, par, half: ffn_act(
                act, i, par, half, sh, SH_TILES, lambda par: sb1_sb, lambda par: sb2_sb[:, 0:1]))
            pipeline(act, SLOT_TILES, 1, 2, lambda act, i, par, half: ffn_act(
                act, i, par, half, ex, SLOT_TILES, lambda par: b_stage[par], lambda par: b_stage[par][:, FC:FC + 1]))

        @block.vector
        def _(dve):
            v = nc.vector
            link = chain(dve, dve_step)

            def stats(b, buf, out_mv, done):
                for t in range(TB):
                    last = v.bn_stats(buf[:, t, :], x_all[:, b * TB + t, :])
                link(last)
                for t in range(TB):
                    last = v.bn_aggr(out_mv[:, t, :], buf[:, t, :])
                last.then_inc(done, 1)

            def stats1_batch(b):
                dve.wait_ge(x_in[b], 16)
                wait(dve, norm1, b)
                stats(b, st, mv, stat1)

            stats1_batch(0)
            dve.wait_ge(comb_ready, 1)
            link(v.tensor_tensor(bcomb[:, :], bank[1][:, 0:3], bqkv_sb[:, :], ALU.add))
            v.tensor_scalar(bcomb[:, 0:1], bcomb[:, 0:1], SCALE, None, ALU.mult).then_inc(comb_b, 1)
            link(v.tensor_copy(rw_hi[:, :], rw_sb[:, :]))
            v.tensor_tensor(rw_lo[:, :], rw_sb[:, :], rw_hi[:, :].bitcast(fp32), ALU.subtract).then_inc(rw_split, 1)
            dve.wait_ge(const_ready, 1)

            def softmax(c):
                dve.wait_ge(scores, c + 1)
                wait(dve, probs_lo, c)
                s = bank[2][:, 0:NEIGH * GT].rearrange("p (n t) -> p n t", n=NEIGH)
                link(v.tensor_reduce(top[:, :], s.rearrange("p n t -> p t n"), X, ALU.max))
                v.tensor_tensor(soft[:, :, :], s, top[:, :].unsqueeze(1).to_broadcast([P, NEIGH, GT]),
                                ALU.subtract).then_inc(shifted, 1)
                dve.wait_ge(exps, c + 1)
                link(v.tensor_reduce(inv[:, :], soft[:, :, :].rearrange("p n t -> p t n"), X, ALU.add))
                link(v.reciprocal(inv[:, :], inv[:, :]))
                v.tensor_tensor(soft[:, :, :], soft[:, :, :], inv[:, :].unsqueeze(1).to_broadcast([P, NEIGH, GT]),
                                ALU.mult).then_inc(probs, 1)
                dve.wait_ge(probs_hi, c + 1)
                v.tensor_tensor(p_lo[:, :, :], soft[:, :, :], p_hi[:, :, :].bitcast(fp32), ALU.subtract)\
                    .then_inc(probs_lo, 1)

            def products(b):
                dve.wait_ge(proj_out, 8 * b + 8)
                dve.wait_ge(halo, b + 1)
                wait(dve, scores, b)
                for n in range(NEIGH):
                    v.tensor_tensor(prod[:, n, :], q_sb, k_sb[:, n:n + SEQ], ALU.mult).then_inc(prod_done, 1)

            def weigh(c):
                for half in range(2):
                    for n in range(NEIGH):
                        use = (2 * c + half) * NEIGH + n
                        dve.wait_ge(spread, use + 1)
                        v.tensor_tensor(weighted[:, n, :], bank[3 + use % 2][:, :],
                                        v_sb[c % 2][:, n + half * 512:n + (half + 1) * 512], ALU.mult)\
                            .then_inc(weighted_v, 1)
                    dve.wait_ge(weighted_v, (2 * c + half + 1) * NEIGH)
                    link(v.tensor_tensor(weighted[:, 0, :], weighted[:, 0, :], weighted[:, 1, :], ALU.add))
                    v.tensor_tensor(attn[:, half * 512:(half + 1) * 512], weighted[:, 0, :], weighted[:, 2, :],
                                    ALU.add).then_inc(attn_done, 1)
                    dve.wait_ge(attn_done, 2 * c + half + 1)

            def residual(c):
                dve.wait_ge(bo_added, c + 1)
                for j in range(2):
                    dve.wait_ge(y_ready, 2 * c + j + 1)
                    part = x_all[:, c * TB + 4 * j:c * TB + 4 * j + 4, :]
                    v.tensor_tensor(part, bank[5 + j][:, :].rearrange("p (t d) -> p t d", d=D), part, ALU.add)\
                        .then_inc(resid, 1)
                dve.wait_ge(resid, 2 * (c + 1))
                wait(dve, norm2, c)
                stats(c, st2, mv2, stat2)
                for j in range(2):
                    dve.wait_ge(xt_hi_done, 2 * c + j + 1)
                    cols = slice(c * SEQ + j * 512, c * SEQ + (j + 1) * 512)
                    v.tensor_tensor(xt_lo[:, cols], bank[5 + j][:, :], xt_hi[:, cols].bitcast(fp32), ALU.subtract)\
                        .then_inc(xt_lo_done, 1)

            def route(c):
                over = lambda m: m[:, :].unsqueeze(2).to_broadcast([P, TB, EXPERTS])
                by_expert = lambda m: m[:, :].unsqueeze(1).to_broadcast([P, TB, EXPERTS])
                tiles = slice(c * TB, (c + 1) * TB)
                dve.wait_ge(logits, c + 1)
                link(v.tensor_tensor(lg[:, :, :], bank[7][:, 0:TB * EXPERTS].rearrange("p (t e) -> p t e", e=EXPERTS),
                                     by_expert(rb_bc), ALU.add))
                for best, sel in ((m1, sel1), (m2, sel2)):
                    link(v.tensor_reduce(best[:, :], lg[:, :, :], X, ALU.max))
                    link(v.tensor_tensor(cand[:, :, :], lg[:, :, :], over(best), ALU.is_ge))
                    link(v.tensor_tensor(cand[:, :, :], cand[:, :, :], by_expert(rank_weight), ALU.mult))
                    link(v.tensor_reduce(km[:, :], cand[:, :, :], X, ALU.max))
                    link(v.tensor_tensor(sel[:, :, :], cand[:, :, :], over(km), ALU.is_equal))
                    if sel is sel1:
                        if c >= 1:
                            dve.wait_ge(scattered, 16 * 2 * TB * c)
                        link(v.tensor_scalar(rows[:, :, D + 1], km[:, :], -1.0, float(EXPERTS), ALU.mult, ALU.add))
                        link(v.scalar_tensor_tensor(lg[:, :, :], sel1[:, :, :], -3.0e38, lg[:, :, :], ALU.mult, ALU.add))
                v.tensor_tensor(either[:, :, :], sel1[:, :, :], sel2[:, :, :], ALU.add).then_inc(chosen, 1)
                v.tensor_tensor(gap[:, :], m2[:, :], m1[:, :], ALU.subtract).then_inc(gap_ready, 1)
                dve.wait_ge(gap_exp, c + 1)
                link(v.tensor_scalar(gate2[:, tiles], eg[:, :], 1.0, None, ALU.add))
                link(v.reciprocal(gate1[:, tiles], gate2[:, tiles]))
                link(v.tensor_tensor(gate2[:, tiles], gate1[:, tiles], eg[:, :], ALU.mult))
                dve.wait_ge(ranks, c + 1)
                link(v.tensor_tensor(slot_at[:, :, :], bank[7][:, 64:64 + TB * EXPERTS].rearrange("p (t e) -> p t e", e=EXPERTS),
                                     by_expert(base), ALU.add))
                link(v.tensor_tensor(base[:, :], bank[7][:, 128:128 + EXPERTS], base[:, :], ALU.add))
                link(v.tensor_tensor(sel1[:, :, :], sel1[:, :, :], slot_at[:, :, :], ALU.mult))
                link(v.tensor_tensor(sel2[:, :, :], sel2[:, :, :], slot_at[:, :, :], ALU.mult))
                with nc.allow_low_precision(reason="row numbers are small integers"):
                    link(v.tensor_reduce(pos1[:, tiles], sel1[:, :, :], X, ALU.add))
                    v.tensor_reduce(pos2[:, tiles], sel2[:, :, :], X, ALU.add).then_inc(routed, 1)
                dve.wait_ge(routed, c + 1)

            stats1_batch(1)
            for b in range(BATCHES + 1):
                if b >= 1:
                    softmax(b - 1)
                if b < BATCHES:
                    products(b)
                if b + 2 < BATCHES:
                    stats1_batch(b + 2)
                if b >= 1:
                    weigh(b - 1)
                    residual(b - 1)
                    route(b - 1)

            link(v.tensor_copy(pad_at[:, :], base[:, :]))
            link(v.tensor_tensor(n_tiles[:, :], base[:, :], region_start[:, :], ALU.subtract))
            link(v.tensor_scalar(n_int[:, :], n_tiles[:, :], float(SLOT - 1), None, ALU.add))
            link(v.tensor_single_scalar(n_int[:, :], n_int[:, :], SLOT.bit_length() - 1, ALU.arith_shift_right))
            link(v.tensor_copy(n_tiles[:, :], n_int[:, :]))
            link(v.tensor_copy(ends[:, 0, 4:], n_int[:, :]))
            for k in range(3):
                link(v.tensor_tensor(ends[:, k + 1, 4:], ends[:, k, 4:], ends[:, k, 4 - (1 << k):4 + EXPERTS - (1 << k)],
                                     ALU.add))
            full = [P, SLOT_TILES, EXPERTS]
            link(v.tensor_tensor(passed, slot_no[:, :].unsqueeze(2).to_broadcast(full),
                                 ends[:, 3, 4:].unsqueeze(1).to_broadcast(full), ALU.is_ge))
            link(v.tensor_reduce(slot_expert[:, :], passed, X, ALU.add))
            link(v.tensor_tensor(passed_n, passed, n_tiles[:, :].unsqueeze(1).to_broadcast(full), ALU.mult))
            link(v.tensor_reduce(n_passed[:, :], passed_n, X, ALU.add))
            link(v.tensor_tensor(n_passed[:, :], slot_no[:, :], n_passed[:, :], ALU.subtract))
            link(v.tensor_scalar(row_f[:, :], slot_expert[:, :], float(REGION), None, ALU.mult))
            link(v.scalar_tensor_tensor(row_f[:, :], n_passed[:, :], float(SLOT), row_f[:, :], ALU.mult, ALU.add))
            link(v.tensor_scalar(slot_row[:, :], row_f[:, :], float(PAD_ROW), None, ALU.min))
            v.tensor_scalar(slot_w[:, :], slot_expert[:, :], float(EXPERTS - 1), None, ALU.min).then_inc(tables, 1)

            def ffn_dve(dve, i, par, half, ph, tiles):
                if ph is ex and runs(i, -1, tiles):
                    k, kpar = i + 1, 1 - par
                    dve.wait_ge(ph.rows_in[kpar], (half + par + 1) * 16)
                    v.scalar_tensor_tensor(y_rows[:, bass.ds(k * SJ, SJ)], xs[kpar][:, :, D + 1],
                                           slot_expert[:, bass.ds(k, 1)], xs[kpar][:, :, D],
                                           ALU.is_equal, ALU.add).then_inc(ph.idx, 1)
                    dve.wait_ge(ph.xs_hi, i + 2)
                    v.tensor_tensor(xs_lo[1 - par], bank[TIN[1 - par]][:, 0:SLOT], xs_hi[1 - par].bitcast(fp32),
                                    ALU.subtract).then_inc(ph.xs_lo, 1)
                if runs(i, 0, tiles):
                    dve.wait_ge(ph.gelu, i + 1)
                    wait(dve, ph.down, i - 1)
                    v.tensor_copy(h_hi[par][:, :, :], h_sb[par]).then_inc(ph.h_hi, 1)
                    dve.wait_ge(ph.h_hi, i + 1)
                    v.tensor_tensor(h_lo[par][:, :, :], h_sb[par], h_hi[par][:, :, :].bitcast(fp32),
                                    ALU.subtract).then_inc(ph.h_lo, 1)
                if runs(i, 2, tiles):
                    k = i - 2
                    dve.wait_ge(ph.tout, k + 1)
                    y = bank[TOUT][:, 0:SLOT].rearrange("p (j d) -> p j d", j=SJ)
                    if ph is ex:
                        wait(dve, ph.y_out[par], (half - 1) * 16 * SJ)
                        v.tensor_copy(y_sb[par], y).then_inc(ph.y, 1)
                    else:
                        part = x_all[:, bass.ds(k * SJ, SJ), :]
                        v.tensor_tensor(part, y, part, ALU.add).then_inc(ph.y, 1)

            pipeline(dve, SH_TILES, 0, 2, lambda dve, i, par, half: ffn_dve(dve, i, par, half, sh, SH_TILES))
            pipeline(dve, SLOT_TILES, 1, 2, lambda dve, i, par, half: ffn_dve(dve, i, par, half, ex, SLOT_TILES))

            dve.wait_ge(sh.y, SH_TILES)
            for g in range(TILES // 4):
                dve.wait_ge(y_in[g % 2], 16 * (g // 2 + 1))
                for k, gate in enumerate((gate2, gate1)):
                    for t in range(4):
                        tile = g * 4 + t
                        ins = v.scalar_tensor_tensor(x_all[:, tile, :], y_back[g % 2][:, t, k * D:(k + 1) * D], gate[:, tile:tile + 1],
                                                     x_all[:, tile, :], ALU.mult, ALU.add)
                    if k == 0:
                        link(ins)
                ins.then_inc(summed, 1)

        @block.tensor
        def _(pe):
            m = nc.tensor
            pe.wait_ge(w_in, W_LOADS)
            m.matmul(bank[0][:, 0:3 * D], wp_sb[:, :], wqkv_sb[:, :], start=True, stop=True)
            for i in range(3):
                last = m.matmul(bank[1][:, i:i + 1], wqkv_sb[:, i * D:(i + 1) * D], bp_sb[:, :], start=True, stop=True)
            last.then_inc(comb_ready, 1)
            pe.wait_ge(comb_w, 1)
            pe.wait_ge(comb_b, 1)

            def project(b):
                for j in range(8):
                    use = 8 * b + j
                    wait(pe, proj_out, use - 1)
                    to = bank[use % 2]
                    if j < 2:
                        pe.wait_ge(norm1, b + 1)
                        for t in range(4):
                            last = m.transpose(to[:, t * D:(t + 1) * D], xn[:, 4 * j + t, :], ident[:, :])
                    else:
                        if j == 2:
                            pe.wait_ge(proj_out, 8 * b + 2)
                        w = (j - 2) // 2
                        last = m.matmul(to[:, :], wcomb[:, w * D:(w + 1) * D], xnt[:, (j % 2) * 512:(j % 2 + 1) * 512],
                                        start=True, stop=True)
                    last.then_inc(proj_ready, 1)

            def score(b):
                pe.wait_ge(prod_done, NEIGH * (b + 1))
                wait(pe, shifted, b)
                for n in range(NEIGH):
                    for grp in range(GROUPS):
                        off = P - HEADS - HEADS * grp
                        last = m.matmul(bank[2][:, n * GT:(n + 1) * GT], score_mask[:, off:off + P],
                                        prod[:, n, grp * GT:(grp + 1) * GT], start=(grp == 0), stop=(grp == GROUPS - 1))
                last.then_inc(scores, 1)

            def spread_probs(c):
                pe.wait_ge(probs_lo, c + 1)
                for half in range(2):
                    for n in range(NEIGH):
                        use = (2 * c + half) * NEIGH + n
                        wait(pe, weighted_v, use - 1)
                        for k in range(4):
                            to = bank[3 + use % 2][:, k * GT:(k + 1) * GT]
                            mask = expand[:, 4 * half + k, :]
                            m.matmul(to, mask, p_hi[:, n, :], start=True, stop=False)
                            last = m.matmul(to, mask, p_lo[:, n, :], start=False, stop=True)
                        last.then_inc(spread, 1)

            def out_project(c):
                for j in range(2):
                    pe.wait_ge(attn_done, 2 * c + j + 1)
                    wait(pe, xt_lo_done, 2 * (c - 1) + j + 1 if c else 0)
                    for t in range(4):
                        tile = 4 * j + t
                        last = m.matmul(bank[5 + j][:, t * D:(t + 1) * D], attn[:, tile * P:(tile + 1) * P], wo_sb[:, :],
                                        start=True, stop=True)
                    last.then_inc(y_ready, 1)

            def transpose2(c):
                pe.wait_ge(norm2, c + 1)
                for j in range(2):
                    for t in range(4):
                        last = m.transpose(bank[5 + j][:, t * D:(t + 1) * D], rows[:, 4 * j + t, 0:D], ident[:, :])
                    last.then_inc(t2_ready, 1)

            def router(c):
                pe.wait_ge(xt_lo_done, 2 * (c + 1))
                pe.wait_ge(rw_split, 1)
                wait(pe, routed, c)
                for t in range(TB):
                    cols = slice((c * TB + t) * P, (c * TB + t + 1) * P)
                    to = bank[7][:, t * EXPERTS:(t + 1) * EXPERTS]
                    m.matmul(to, xt_hi[:, cols], rw_hi[:, :], start=True, stop=False)
                    m.matmul(to, xt_hi[:, cols], rw_lo[:, :], start=False, stop=False)
                    last = m.matmul(to, xt_lo[:, cols], rw_hi[:, :], start=False, stop=True)
                last.then_inc(logits, 1)

            def rank(c):
                pe.wait_ge(chosen, c + 1)
                to = bank[7][:, 64:64 + TB * EXPERTS].rearrange("p (t e) -> p t e", e=EXPERTS)
                m.matmul(to, before[:, :], either[:, :, :], start=True, stop=False, skip_group_check=True)
                for back in range(1, TB):
                    m.matmul(to[:, back:, :], ones_bf[:, :], either[:, 0:TB - back, :], start=False,
                             stop=(back == TB - 1), skip_group_check=True)
                for t in range(TB):
                    last = m.matmul(bank[7][:, 128:128 + EXPERTS], ones_bf[:, :], either[:, t, :],
                                    start=(t == 0), stop=(t == TB - 1), skip_group_check=True)
                last.then_inc(ranks, 1)

            for b in range(BATCHES + 1):
                if b < BATCHES:
                    project(b)
                if b >= 1:
                    spread_probs(b - 1)
                if b < BATCHES:
                    score(b)
                if b >= 1:
                    out_project(b - 1)
                    transpose2(b - 1)
                    router(b - 1)
                    rank(b - 1)

            def ffn_pe(pe, i, par, half, ph, tiles, w_of, hi_of, lo_of):
                if ph is ex and runs(i, -1, tiles):
                    k, kpar, khalf = i + 1, 1 - par, half + par
                    pe.wait_ge(ph.rows_in[kpar], (khalf + 1) * 16)
                    wait(pe, ph.xs_lo, k - 1)
                    for j in range(SJ):
                        last = m.transpose(bank[TIN[kpar]][:, j * P:(j + 1) * P], xs[kpar][:, j, 0:D], ident[:, :])
                    last.then_inc(ph.tin, 1)
                if runs(i, 0, tiles):
                    w = w_of(par)
                    if ph is ex:
                        pe.wait_ge(ph.w_in[par], (half + 1) * 32)
                        pe.wait_ge(ph.xs_lo, i + 1)
                    wait(pe, ph.gelu, i - 1)
                    hi, lo = hi_of(i, par), lo_of(i, par)
                    for c in range(FC):
                        to = bank[2 * par + c // 2][:, (c % 2) * SLOT:(c % 2 + 1) * SLOT]
                        w_hi, w_lo = w[:, 0, c * P:(c + 1) * P], w[:, 1, c * P:(c + 1) * P]
                        m.matmul(to, w_hi, hi, start=True, stop=False)
                        m.matmul(to, w_hi, lo, start=False, stop=False)
                        last = m.matmul(to, w_lo, hi, start=False, stop=True)
                    last.then_inc(ph.up, 1)
                if runs(i, 1, tiles):
                    w = w_of(1 - par)
                    pe.wait_ge(ph.h_lo, i)
                    wait(pe, ph.yt, i - 1)
                    to = bank[DOWN][:, 0:SLOT]
                    for c in range(FC):
                        w_hi, w_lo = w[:, 2, c * P:(c + 1) * P], w[:, 3, c * P:(c + 1) * P]
                        h, l = h_hi[1 - par][:, c, :], h_lo[1 - par][:, c, :]
                        m.matmul(to, w_hi, h, start=(c == 0), stop=False)
                        m.matmul(to, w_hi, l, start=False, stop=False)
                        last = m.matmul(to, w_lo, h, start=False, stop=(c == FC - 1))
                    last.then_inc(ph.down, 1)
                if runs(i, 2, tiles):
                    pe.wait_ge(ph.yt, i - 1)
                    wait(pe, ph.y, i - 2)
                    for j in range(SJ):
                        last = m.transpose(bank[TOUT][:, j * P:(j + 1) * P], yt[par][:, j * P:(j + 1) * P], ident[:, :])
                    last.then_inc(ph.tout, 1)

            pe.wait_ge(raw_hi, 2)
            pe.wait_ge(raw_lo, 2)
            pe.wait_ge(routed, BATCHES)
            pipeline(pe, SH_TILES, 0, 2, lambda pe, i, par, half: ffn_pe(
                pe, i, par, half, sh, SH_TILES, lambda par: sw,
                lambda i, par: xt_hi[:, bass.ds(i * SLOT, SLOT)], lambda i, par: xt_lo[:, bass.ds(i * SLOT, SLOT)]))
            pipeline(pe, SLOT_TILES, 1, 2, lambda pe, i, par, half: ffn_pe(
                pe, i, par, half, ex, SLOT_TILES, lambda par: stage[par],
                lambda i, par: xs_hi[par], lambda i, par: xs_lo[par]))

    return nc


def kernel(**inputs):
    import numpy as np
    import concourse.bacc as bacc
    from concourse.bass_utils import run_bass_kernel_spmd

    p = {k.replace("L0_", ""): np.asarray(v) for k, v in inputs.items()}
    t = lambda a: np.ascontiguousarray(np.swapaxes(a, -1, -2))
    chunks = lambda a: np.ascontiguousarray(a.reshape(a.shape[:-1] + (-1, P)).swapaxes(-1, -2))
    arrays = {
        "x": p["attn_x"],
        "wp": p["attn_Wp"],
        "bp": p["attn_bp"],
        "wqkv_t": np.concatenate([t(p["attn_Wq"]), t(p["attn_Wk"]), t(p["attn_Wv"])], axis=1),
        "bqkv": t(np.stack([p["attn_bq"], p["attn_bk"], p["attn_bv"]])),
        "wo_t": t(p["attn_Wo"]),
        "bo": p["attn_bo"],
        "sw1_t": t(p["ffn_shared_w1"]),
        "sb1": chunks(p["ffn_shared_b1"]),
        "sw2_t": t(p["ffn_shared_w2"]),
        "sb2": p["ffn_shared_b2"],
        "rw_t": t(p["ffn_router_w"]),
        "rb": p["ffn_router_b"],
        "ew1_t": t(p["ffn_spec_w1"]),
        "ew2_t": t(p["ffn_spec_w2"]),
        "eb": np.concatenate([chunks(p["ffn_spec_b1"]).swapaxes(0, 1), t(p["ffn_spec_b2"])[:, :, None]], axis=2),
    }
    nc = bacc.Bacc("TRN2", target_bir_lowering=False, num_devices=1)
    args = {}
    for name, a in arrays.items():
        arrays[name] = a = np.ascontiguousarray(a)
        args[name] = nc.dram_tensor(name, a.shape, mybir.dt.from_np(a.dtype), kind="ExternalInput").ap()
    out = nc.dram_tensor("out", (BATCHES, SEQ, D), mybir.dt.float32, kind="ExternalOutput").ap()
    preln_local_attention_moe(nc, **args, out=out)
    r = run_bass_kernel_spmd(nc, [arrays], core_ids=[0])
    return r.results[0]["out"]
```

```python
import concourse.bass as bass
from concourse import mybir
from contextlib import ExitStack

P = 128
BATCHES, SEQ, D = 4, 1024, 128
TOKENS = BATCHES * SEQ
HEADS = 16
HEAD_DIM = D // HEADS
NEIGH = 3
FF = 512
FC = FF // P
EXPERTS = 8
EPS = 1e-5

TB = SEQ // P
TILES = TOKENS // P
GROUPS = P // HEADS
GT = SEQ // GROUPS

SLOT = 512
SJ = SLOT // P
REGION = TOKENS + SLOT
PAD_ROW = EXPERTS * REGION
XG_ROWS = PAD_ROW + SLOT
ROW = D + 2
SLOT_TILES = 2 * TOKENS // SLOT + EXPERTS - 1
PAD_TOKEN = 4 * TOKENS
SH_TILES = TOKENS // SLOT


def preln_local_attention_moe(nc, x, wp, bp, wqkv_t, bqkv, wo_t, bo, sw1_t, sb1, sw2_t, sb2, rw_t, rb,
                              ew1_t, ew2_t, eb, out):
    fp32, fp32r = mybir.dt.float32, mybir.dt.float32r
    bf16, int32 = mybir.dt.bfloat16, mybir.dt.int32
    ALU = mybir.AluOpType
    ACT = mybir.ActivationFunctionType
    X = mybir.AxisListType.X
    SCALE = float(HEAD_DIM) ** -0.5

    xg = nc.dram_tensor("rows_by_expert", (XG_ROWS, ROW), fp32, kind="Internal").ap()
    yg = nc.dram_tensor("expert_outputs", (2 * TOKENS, D), fp32, kind="Internal").ap()

    with ExitStack() as ctx:
        def sb(name, shape, dt=fp32):
            return ctx.enter_context(nc.sbuf_tensor(name, shape, dt))

        def sem(name):
            return ctx.enter_context(nc.semaphore(name))

        bank = [ctx.enter_context(nc.psum_tensor(f"bank{i}", [P, 512], fp32)) for i in range(8)]

        ident = sb("ident", [P, P])
        score_mask = sb("score_mask", [P, 2 * P - HEADS])
        expand = sb("expand", [P, GROUPS, P], fp32r)
        before = sb("before", [P, P], bf16)
        ones_bf = sb("ones_bf", [P, P], bf16)
        rank_weight = sb("rank_weight", [P, EXPERTS])
        region_start = sb("region_start", [P, EXPERTS])
        half_neg = sb("half_neg", [P, TILES])
        slot_no = sb("slot_no", [P, SLOT_TILES])

        wp_sb = sb("wp_sb", [P, D])
        wqkv_sb = sb("wqkv_sb", [P, 3 * D])
        wcomb = sb("wcomb", [P, 3 * D])
        bp_sb = sb("bp_sb", [P, 1])
        bqkv_sb = sb("bqkv_sb", [P, 3])
        bcomb = sb("bcomb", [P, 3])
        wo_sb = sb("wo_sb", [P, D])
        bo_bc = sb("bo_bc", [P, D])
        rw_sb = sb("rw_sb", [P, EXPERTS])
        rw_hi = sb("rw_hi", [P, EXPERTS], fp32r)
        rw_lo = sb("rw_lo", [P, EXPERTS], fp32r)
        rb_bc = sb("rb_bc", [P, EXPERTS])

        x_all = sb("x_all", [P, TILES, D])
        rows = [sb(f"rows{i}", [P, TB, ROW]) for i in range(2)]
        xt_hi = sb("xt_hi", [P, TOKENS], fp32r)
        xt_lo = sb("xt_lo", [P, TOKENS], fp32r)
        gate1 = sb("gate1", [P, TILES])
        gate2 = sb("gate2", [P, TILES])
        pos1 = sb("pos1", [P, TILES], int32)
        pos2 = sb("pos2", [P, TILES], int32)

        w_all = sb("w_all", [P, EXPERTS, 4, FF], fp32r)
        b_all = sb("b_all", [P, EXPERTS, FC + 1])
        b_tile = sb("b_tile", [P, SLOT_TILES, FC + 1])
        sb1_sb = sb("sb1_sb", [P, FC])
        sb2_sb = sb("sb2_sb", [P, 1])

        w_raw = sb("w_raw", [P, FF])
        sw = sb("sw", [P, 4, FF], fp32r)
        h_hi = sb("h_hi", [P, FC, SLOT], fp32r)
        h_lo = sb("h_lo", [P, FC, SLOT], fp32r)
        stage = [xt_hi[:, i * 4 * FF:(i + 1) * 4 * FF].rearrange("p (w f) -> p w f", w=4) for i in range(2)]
        xs_hi = [xt_lo[:, i * 2 * SLOT:(i * 2 + 1) * SLOT] for i in range(2)]
        xs_lo = [xt_lo[:, (i * 2 + 1) * SLOT:(i + 1) * 2 * SLOT] for i in range(2)]

        ARENA = 2 * SEQ + NEIGH * 512 + 3 * (SEQ + 2) + NEIGH * SEQ
        arena = sb("arena", [P, ARENA])
        at = [0]

        def piece(n):
            at[0] += n
            assert at[0] <= ARENA
            return arena[:, at[0] - n:at[0]]

        xn = piece(TB * D).rearrange("p (t d) -> p t d", d=D)
        xnt = piece(SEQ)
        piece(NEIGH * 512 - SEQ)
        weighted = arena[:, TB * D:TB * D + NEIGH * 512].rearrange("p (n t) -> p n t", n=NEIGH)
        q_sb = piece(SEQ)
        k_sb = piece(SEQ + 2)
        v_sb = [piece(SEQ + 2) for _ in range(2)]
        prod = piece(NEIGH * SEQ).rearrange("p (n t) -> p n t", n=NEIGH)
        expand_raw = prod[:, 0, :]
        at[0] = 0
        h_sb = piece(FC * SLOT).rearrange("p (c t) -> p c t", c=FC)
        yt = [piece(SLOT) for _ in range(2)]
        y_sb = [piece(SLOT).rearrange("p (j d) -> p j d", j=SJ) for _ in range(2)]
        xs = [piece(SJ * ROW).rearrange("p (j d) -> p j d", j=SJ) for _ in range(2)]
        pad_rows = piece(SJ * ROW).rearrange("p (j d) -> p j d", j=SJ)
        passed = piece(SLOT_TILES * EXPERTS).rearrange("p (s e) -> p s e", e=EXPERTS)
        passed_n = piece(SLOT_TILES * EXPERTS).rearrange("p (s e) -> p s e", e=EXPERTS)
        at[0] -= SJ * ROW + 2 * SLOT_TILES * EXPERTS
        y_back = [piece(2 * 4 * D).rearrange("p (t kd) -> p t kd", t=4) for _ in range(2)]

        st = sb("st", [P, TB, 6])
        mv = sb("mv", [P, TILES, 2])
        rstd = sb("rstd", [P, TILES])
        shift = sb("shift", [P, TILES])
        st2 = sb("st2", [P, TB, 6])
        mv2 = sb("mv2", [P, TB, 2])
        rstd2 = sb("rstd2", [P, TB])
        newton = sb("newton", [P, TB])
        shift2 = sb("shift2", [P, TB])
        top = sb("top", [P, GT])
        soft = sb("soft", [P, NEIGH, GT])
        p_hi = sb("p_hi", [P, NEIGH, GT], fp32r)
        p_lo = sb("p_lo", [P, NEIGH, GT], fp32r)
        inv = sb("inv", [P, GT])

        lg = sb("lg", [P, TB, EXPERTS])
        cand = sb("cand", [P, TB, EXPERTS])
        sel1 = sb("sel1", [P, TB, EXPERTS])
        sel2 = sb("sel2", [P, TB, EXPERTS])
        either = sb("either", [P, TB, EXPERTS], bf16)
        m1 = sb("m1", [P, TB])
        m2 = sb("m2", [P, TB])
        km = sb("km", [P, TB])
        eg = sb("eg", [P, TB])
        gap = sb("gap", [P, TB])
        slot_at = sb("slot_at", [P, TB, EXPERTS])
        base = sb("base", [P, EXPERTS])

        n_int = sb("n_int", [P, EXPERTS], int32)
        n_tiles = sb("n_tiles", [P, EXPERTS])
        ends = sb("ends", [P, 4, 4 + EXPERTS])
        pad_at = sb("pad_at", [P, EXPERTS], int32)
        slot_expert = sb("slot_expert", [P, SLOT_TILES])
        n_passed = sb("n_passed", [P, SLOT_TILES])
        row_f = sb("row_f", [P, SLOT_TILES])
        row_of = sb("row_of", [P, SLOT_TILES])
        slot_row = sb("slot_row", [P, SLOT_TILES], int32)
        slot_w = sb("slot_w", [P, SLOT_TILES], int32)
        y_rows = sb("y_rows", [P, SJ * SLOT_TILES], int32)
        y_row = [sb(f"y_row{i}", [P, SJ], int32) for i in range(2)]

        TIN, DOWN, TOUT = 4, 5, 6
        W_LOADS = 16 * 8
        out_view = lambda g: out.rearrange("b s d -> (b s) d")[g * 4 * P:(g + 1) * 4 * P, :].rearrange(
            "(t p) d -> p t d", p=P)

        x_in = [sem(f"x_in{b}") for b in range(BATCHES)]
        w_in = sem("w_in")
        bias_in = sem("bias_in")
        raw_in = sem("raw_in")
        raw_hi = sem("raw_hi")
        raw_lo = sem("raw_lo")
        const_ready = sem("const_ready")
        pool_step, dve_step, act_step = sem("pool_step"), sem("dve_step"), sem("act_step")
        comb_ready = sem("comb_ready")
        comb_w = sem("comb_w")
        comb_b = sem("comb_b")
        stat1, norm1 = sem("stat1"), sem("norm1")
        bo_added = sem("bo_added")
        proj_ready = sem("proj_ready")
        proj_out = sem("proj_out")
        halo = sem("halo")
        prod_done = sem("prod_done")
        scores = sem("scores")
        shifted = sem("shifted")
        exps = sem("exps")
        probs, probs_hi, probs_lo = sem("probs"), sem("probs_hi"), sem("probs_lo")
        spread = sem("spread")
        weighted_v = sem("weighted_v")
        pow1, shift1_done = sem("pow1"), sem("shift1_done")
        var2, rough2, shift2_done = sem("var2"), sem("rough2"), sem("shift2_done")
        pad_ready = sem("pad_ready")
        y_ready = sem("y_ready")
        resid = sem("resid")
        stat2, norm2 = sem("stat2"), sem("norm2")
        t2_ready = sem("t2_ready")
        xt_hi_done, xt_lo_done = sem("xt_hi_done"), sem("xt_lo_done")
        rw_split = sem("rw_split")
        logits = sem("logits")
        chosen = sem("chosen")
        ranks = sem("ranks")
        gap_ready, gap_exp = sem("gap_ready"), sem("gap_exp")
        routed = sem("routed")
        scattered = [sem(f"scattered{c}") for c in range(BATCHES)]
        tables = sem("tables")
        pad_out = sem("pad_out")
        y_in = [sem(f"y_in{i}") for i in range(2)]
        summed = sem("summed")
        out_done = sem("out_done")

        class Phase:
            def __init__(self, name):
                self.rows_in = [sem(f"{name}_rows_in{i}") for i in range(2)]
                self.w_in = [[sem(f"{name}_w{layer}_in{i}") for i in range(2)] for layer in (1, 2)]
                self.tin = sem(f"{name}_tin")
                self.xs_hi = sem(f"{name}_xs_hi")
                self.xs_lo = sem(f"{name}_xs_lo")
                self.up = sem(f"{name}_up")
                self.gelu = sem(f"{name}_gelu")
                self.h_hi = sem(f"{name}_h_hi")
                self.h_lo = sem(f"{name}_h_lo")
                self.down = sem(f"{name}_down")
                self.yt = sem(f"{name}_yt")
                self.tout = sem(f"{name}_tout")
                self.y = sem(f"{name}_y")
                self.idx = sem(f"{name}_idx")
                self.row, self.go = sem(f"{name}_row"), sem(f"{name}_go")
                self.y_out = [sem(f"{name}_y_out{i}") for i in range(2)]

        sh, ex = Phase("sh"), Phase("ex")

        block = ctx.enter_context(nc.Block())

        def chain(eng, signal):
            n = [0]

            def link(ins):
                n[0] += 1
                ins.then_inc(signal, 1)
                eng.wait_ge(signal, n[0])
            return link

        def wait(eng, signal, value):
            if not isinstance(value, int) or value > 0:
                eng.wait_ge(signal, value)

        def steady(eng, first, last, step):
            assert first % 2 == 0 and (last - first) % 2 == 1
            with eng.Fori(0, (last - first + 1) // 2) as pair:
                for par in range(2):
                    step(eng, pair * 2 + (first + par), par, pair + first // 2)

        def pipeline(eng, tiles, ahead, behind, step):
            first, last = behind + behind % 2, tiles - 1 - ahead
            if (last - first) % 2 == 0:
                last -= 1
            for i in range(-ahead, first):
                step(eng, i, i % 2, i // 2)
            steady(eng, first, last, step)
            for i in range(last + 1, tiles + behind):
                step(eng, i, i % 2, i // 2)

        def runs(i, back, tiles):
            return not isinstance(i, int) or 0 <= i - back < tiles

        WEIGHT_PIECES = 2 * (EXPERTS + 1)
        PIECES_AT = [3] * (BATCHES + 2)

        def raw_piece(n):
            if n < 2:
                src, dst = (sw1_t, sw2_t)[n], sw
                e = None
            else:
                e = (n - 2) // 2
                src, dst = (ew1_t, ew2_t)[n % 2][e], w_all[:, e]
            dst = sw[:, :, :] if e is None else w_all[:, e, :, :]
            return src, dst[:, 2 * (n % 2), :], dst[:, 2 * (n % 2) + 1, :]

        @block.sync
        def _(sp):
            for b in range(BATCHES):
                sp.dma_start(x_all[:, b * TB:(b + 1) * TB, :],
                             x[b].rearrange("(t p) d -> p t d", p=P)).then_inc(x_in[b], 16)
            for n in range(WEIGHT_PIECES):
                wait(sp, raw_lo, n)
                src = raw_piece(n)[0]
                if n % 2:
                    sp.dma_start(w_raw[:, :].rearrange("p (c d) -> p c d", c=FC),
                                 src.rearrange("(c p) d -> p c d", p=P)).then_inc(raw_in, 16)
                else:
                    sp.dma_start(w_raw[:, :], src).then_inc(raw_in, 16)

            sp.wait_ge(tables, 1)
            sp.wait_ge(pad_ready, 1)
            for e in range(EXPERTS):
                row = sp.value_load(pad_at[0:1, e:e + 1], min_val=e * REGION, max_val=e * REGION + TOKENS)
                sp.dma_start(xg[bass.ds(row, SLOT), :].rearrange("(j p) c -> p j c", p=P),
                             pad_rows).then_inc(pad_out, 16)
            sp.dma_start(xg[PAD_ROW:PAD_ROW + SLOT, :].rearrange("(j p) c -> p j c", p=P),
                         pad_rows).then_inc(pad_out, 16)
            sp.wait_ge(pad_out, 16 * (EXPERTS + 1))
            for c in range(BATCHES):
                sp.wait_ge(scattered[c], 16 * 2 * TB)
            sp.wait_ge(raw_lo, WEIGHT_PIECES)
            sp.wait_ge(raw_hi, WEIGHT_PIECES)
            sp.wait_ge(sh.up, FC * SH_TILES)

            def load_tile(sp, i, par, half):
                if runs(i, -2, SLOT_TILES):
                    k = i + 2
                    wait(sp, ex.tin, k - 1)
                    wait(sp, ex.idx, k - 1)
                    row = sp.value_load(slot_row[0:1, bass.ds(k, 1)], min_val=0, max_val=PAD_ROW)
                    sp.dma_start(xs[par], xg[bass.ds(row, SLOT), :].rearrange("(j p) c -> p j c", p=P))\
                        .then_inc(ex.rows_in[par], 16)
                if runs(i, -1, SLOT_TILES):
                    k = i + 1
                    e = sp.value_load(slot_w[0:1, bass.ds(k, 1)], min_val=0, max_val=EXPERTS - 1)
                    for layer, used in enumerate((ex.up, ex.down)):
                        wait(sp, used, FC * (k - 1))
                        sp.dma_start(stage[1 - par][:, 2 * layer:2 * layer + 2, :].bitcast(fp32),
                                     w_all[:, bass.ds(e, 1), 2 * layer:2 * layer + 2, :]
                                     .rearrange("p a w f -> p (a w) f").bitcast(fp32))\
                            .then_inc(ex.w_in[layer][1 - par], 16)
            pipeline(sp, SLOT_TILES, 2, 0, load_tile)

            for par in range(2):
                sp.wait_ge(ex.y_out[par], 16 * SJ * ((SLOT_TILES + 1 - par) // 2))
            for g in range(TILES // 4):
                wait(sp, summed, g - 1)
                sp.dma_start(y_back[g % 2], yg[g * 8 * P:(g + 1) * 8 * P, :]
                             .rearrange("(t p k) d -> p t (k d)", p=P, k=2)).then_inc(y_in[g % 2], 16)
                if g >= 1:
                    sp.wait_ge(summed, g)
                    sp.dma_start(out_view(g - 1), x_all[:, (g - 1) * 4:g * 4, :]).then_inc(out_done, 16)
            sp.wait_ge(summed, TILES // 4)
            sp.dma_start(out_view(TILES // 4 - 1), x_all[:, TILES - 4:TILES, :]).then_inc(out_done, 16)
            sp.wait_ge(out_done, 16 * (TILES // 4))

        @block.gpsimd
        def _(pool):
            link = chain(pool, pool_step)
            g = nc.gpsimd
            link(g.memset(ident[:, :], 0.0))
            link(g.affine_select(out=ident[:, :], in_=ident[:, :], compare_op=ALU.not_equal, fill=1.0,
                                 base=0, pattern=[[-1, P]], channel_multiplier=1))
            link(g.memset(half_neg[:, :], -0.5))

            def add_bo(b):
                pool.wait_ge(norm1, b + 1)
                pool.wait_ge(w_in, W_LOADS)
                xb = x_all[:, b * TB:(b + 1) * TB, :]
                g.tensor_tensor(xb, xb, bo_bc[:, :].unsqueeze(1).to_broadcast([P, TB, D]), ALU.add)\
                    .then_inc(bo_added, 1)

            def weight_lo(n):
                _, hi, lo = raw_piece(n)
                pool.wait_ge(raw_hi, n + 1)
                g.tensor_tensor(lo, w_raw[:, :], hi.bitcast(fp32), ALU.subtract).then_inc(raw_lo, 1)

            def scale1(b):
                cols = slice(b * TB, (b + 1) * TB)
                pool.wait_ge(stat1, b + 1)
                link(g.tensor_scalar_add(rstd[:, cols], mv[:, cols, 1], EPS))
                g.tensor_tensor(rstd[:, cols], rstd[:, cols], half_neg[:, cols], ALU.pow).then_inc(pow1, 1)

            scale1(0)
            link(g.memset(score_mask[:, :], 1.0))
            link(g.affine_select(out=score_mask[:, :], in_=score_mask[:, :], compare_op=ALU.is_ge, fill=0.0,
                                 base=HEAD_DIM * (P - HEADS), pattern=[[-HEAD_DIM, 2 * P - HEADS]],
                                 channel_multiplier=1))
            link(g.affine_select(out=score_mask[:, :], in_=score_mask[:, :], compare_op=ALU.is_ge, fill=0.0,
                                 base=HEAD_DIM - 1 - HEAD_DIM * (P - HEADS),
                                 pattern=[[HEAD_DIM, 2 * P - HEADS]], channel_multiplier=-1))
            link(g.memset(expand_raw[:, :], 0.0))
            link(g.affine_select(out=expand_raw[:, :], in_=expand_raw[:, :], compare_op=ALU.not_equal,
                                 fill=1.0, base=0, pattern=[[-HEADS, GROUPS], [-1, HEADS], [0, HEAD_DIM]],
                                 channel_multiplier=1))
            link(g.tensor_copy(expand[:, :, :].rearrange("p g d -> p (g d)"), expand_raw[:, :]))
            link(g.memset(ones_bf[:, :], 1.0))
            link(g.affine_select(out=before[:, :], in_=ones_bf[:, :], compare_op=ALU.is_gt, fill=0.0,
                                 base=0, pattern=[[1, P]], channel_multiplier=-1))
            link(g.iota(rank_weight[:, :], pattern=[[-1, EXPERTS]], base=EXPERTS, channel_multiplier=0,
                        allow_small_or_imprecise_dtypes=True))
            link(g.iota(region_start[:, :], pattern=[[REGION, EXPERTS]], base=0, channel_multiplier=0,
                        allow_small_or_imprecise_dtypes=True))
            link(g.tensor_copy(base[:, :], region_start[:, :]))
            link(g.iota(slot_no[:, :], pattern=[[1, SLOT_TILES]], base=0, channel_multiplier=0,
                        allow_small_or_imprecise_dtypes=True))
            g.memset(ends[:, :, :], 0.0).then_inc(const_ready, 1)
            for b in range(1, BATCHES):
                scale1(b)

            pieces = iter(range(WEIGHT_PIECES))
            for b in range(BATCHES + 2):
                if b < BATCHES:
                    add_bo(b)
                for _ in range(PIECES_AT[b]):
                    weight_lo(next(pieces))
                if b >= 2:
                    c = b - 2
                    if c >= 2:
                        pool.wait_ge(scattered[c - 2], 16 * 2 * TB)
                    link(g.iota(rows[c % 2][:, :, D:D + 1], pattern=[[2 * P, TB], [0, 1]], base=2 * c * SEQ,
                                channel_multiplier=2, allow_small_or_imprecise_dtypes=True))
                    pool.wait_ge(norm2, c + 1)
                    pool.wait_ge(routed, c + 1)
                    if c == BATCHES - 1:
                        link(g.memset(pad_rows, 0.0))
                        link(g.memset(pad_rows[:, :, D:D + 1], float(PAD_TOKEN)))
                        g.memset(pad_rows[:, :, D + 1:D + 2], -1.0).then_inc(pad_ready, 1)
                    for t in range(TB):
                        for pos in (pos1, pos2):
                            g.indirect_dma_start(
                                xg[:, :], bass.IndirectOffsetOnAxis(ap=pos[:, c * TB + t:c * TB + t + 1], axis=0),
                                rows[c % 2][:, t, :], None).then_inc(scattered[c], 16)
            pool.wait_ge(tables, 1)

            last_row = pool.to_reg(2 * TOKENS - 1)

            def put_tile(pool, i, par, half):
                k = i - 2
                if runs(i, 2, SLOT_TILES):
                    wait(pool, ex.y_out[par], (half - 1) * 16 * SJ)
                    pool.wait_ge(ex.idx, k + 1)
                    g.tensor_copy(y_row[par][:, :], y_rows[:, bass.ds(k * SJ, SJ)]).then_inc(ex.row, 1)
                    pool.wait_ge(ex.row, k + 1)
                    pool.wait_ge(ex.y, k + 1)
                    pool.sem_inc(ex.go, 1)
                    for j in range(SJ):
                        g.indirect_dma_start(
                            yg[:, :], bass.IndirectOffsetOnAxis(ap=y_row[par][:, j:j + 1], axis=0),
                            y_sb[par][:, j, :], None, bounds_check=last_row, oob_is_err=False)\
                            .then_inc(ex.y_out[par], 16)
            pipeline(pool, SLOT_TILES, 0, 2, put_tile)

        @block.scalar
        def _(act):
            a = nc.scalar
            act.dma_start(wp_sb[:, :], wp).then_inc(w_in, 16)
            act.dma_start(wqkv_sb[:, :], wqkv_t).then_inc(w_in, 16)
            act.dma_start(bp_sb[:, :], bp.rearrange("(p a) -> p a", a=1)).then_inc(w_in, 16)
            act.dma_start(bqkv_sb[:, :], bqkv).then_inc(w_in, 16)
            act.dma_start(wo_sb[:, :], wo_t).then_inc(w_in, 16)
            act.dma_start(rw_sb[:, :], rw_t).then_inc(w_in, 16)
            act.dma_start(bo_bc[:, :], bo.rearrange("(a n) -> a n", a=1).to_broadcast([P, D])).then_inc(w_in, 16)
            act.dma_start(rb_bc[:, :], rb.rearrange("(a n) -> a n", a=1).to_broadcast([P, EXPERTS])).then_inc(w_in, 16)
            act.dma_start(sb1_sb[:, :], sb1).then_inc(bias_in, 16)
            act.dma_start(sb2_sb[:, :], sb2.rearrange("(p a) -> p a", a=1)).then_inc(bias_in, 16)
            act.dma_start(b_all[:, :, :], eb).then_inc(bias_in, 16)

            act.wait_ge(comb_ready, 1)
            a.activation(wcomb[:, :], bank[0][:, 0:3 * D], ACT.Copy).then_inc(comb_w, 1)

            def transposed2(act, a, c):
                if 0 <= c < BATCHES:
                    for j in range(2):
                        act.wait_ge(t2_ready, 2 * c + j + 1)
                        a.activation(xt_hi[:, c * SEQ + j * 512:c * SEQ + (j + 1) * 512], bank[5 + j][:, :],
                                     ACT.Copy).then_inc(xt_hi_done, 1)

            def probs_high(act, a, c):
                if 0 <= c < BATCHES:
                    act.wait_ge(probs, c + 1)
                    wait(act, spread, 2 * NEIGH * c)
                    a.activation(p_hi[:, :, :], soft[:, :, :], ACT.Copy).then_inc(probs_hi, 1)

            def weight_hi(n):
                _, hi, _ = raw_piece(n)
                act.wait_ge(raw_in, 16 * (n + 1))
                a.activation(hi, w_raw[:, :], ACT.Copy).then_inc(raw_hi, 1)

            def norm(b, src_tile, r, sh, dst, done):
                for t in range(TB):
                    last = a.activation(dst[:, t, 0:D], x_all[:, b * TB + t, :], ACT.Identity,
                                        bias=sh[:, src_tile + t:src_tile + t + 1],
                                        scale=r[:, src_tile + t:src_tile + t + 1])
                last.then_inc(done, 1)

            def norm1_batch(b):
                wait(act, proj_ready, 8 * (b - 1) + 2 if b else 0)
                act.wait_ge(shift1_done, b + 1)
                norm(b, b * TB, rstd, shift, xn, norm1)

            pieces = iter(range(WEIGHT_PIECES))
            norm1_batch(0)
            use = 0
            for b in range(BATCHES + 2):
                c = b - 1
                if 0 <= c < BATCHES:
                    act.wait_ge(shifted, c + 1)
                    a.activation(soft[:, :, :], soft[:, :, :], ACT.Exp).then_inc(exps, 1)
                if b < BATCHES:
                    targets = [(xnt, None)] * 2 + [(q_sb, 0)] * 2 + [(k_sb[:, 1:], 1)] * 2 + [(v_sb[b % 2][:, 1:], 2)] * 2
                else:
                    targets = []
                for j, (dst, which) in enumerate(targets):
                    if j == 0:
                        wait(act, y_ready, 2 * (b - 1))
                    if j == 2:
                        transposed2(act, a, b - 2)
                        probs_high(act, a, b - 1)
                        wait(act, prod_done, NEIGH * b)
                    if j == 6:
                        wait(act, weighted_v, 2 * NEIGH * (b - 1))
                    act.wait_ge(proj_ready, use + 1)
                    dst = dst[:, (j % 2) * 512:(j % 2 + 1) * 512]
                    if which is None:
                        a.activation(dst, bank[use % 2][:, :], ACT.Copy).then_inc(proj_out, 1)
                    else:
                        a.activation(dst, bank[use % 2][:, :], ACT.Identity, bias=bcomb[:, which:which + 1],
                                     scale=SCALE if which == 0 else 1.0).then_inc(proj_out, 1)
                    use += 1
                if b < BATCHES:
                    act.wait_ge(proj_out, use)
                    for buf in (k_sb, v_sb[b % 2]):
                        a.activation(buf[:, 0:1], buf[:, SEQ:SEQ + 1], ACT.Copy)
                        last = a.activation(buf[:, SEQ + 1:SEQ + 2], buf[:, 1:2], ACT.Copy)
                    last.then_inc(halo, 1)
                else:
                    transposed2(act, a, b - 2)
                    probs_high(act, a, b - 1)
                if b + 1 < BATCHES:
                    norm1_batch(b + 1)
                for _ in range(PIECES_AT[b]):
                    weight_hi(next(pieces))
                if b >= 2:
                    act.wait_ge(gap_ready, b - 1)
                    a.activation(eg[:, :], gap[:, :], ACT.Exp).then_inc(gap_exp, 1)
                if 0 <= c < BATCHES:
                    act.wait_ge(var2, c + 1)
                    a.activation(newton[:, :], rstd2[:, :], ACT.Ln).then_inc(act_step, 1)
                    act.wait_ge(act_step, c + 1)
                    a.activation(newton[:, :], newton[:, :], ACT.Exp, scale=-0.5).then_inc(rough2, 1)
                    act.wait_ge(shift2_done, c + 1)
                    if c >= 2:
                        act.wait_ge(scattered[c - 2], 16 * 2 * TB)
                        act.wait_ge(t2_ready, 2 * (c - 1))
                    norm(c, 0, rstd2, shift2, rows[c % 2], norm2)
            act.wait_ge(bias_in, 16 * 3)

            def ffn_act(act, i, par, half, ph, tiles, b1_of, b2_of):
                if ph is ex and runs(i, -1, tiles):
                    k = i + 1
                    act.wait_ge(ph.tin, k + 1)
                    wait(act, ph.up, FC * (k - 1))
                    a.activation(xs_hi[1 - par], bank[TIN][:, :], ACT.Copy).then_inc(ph.xs_hi, 1)
                if runs(i, 0, tiles):
                    for c in range(FC):
                        act.wait_ge(ph.up, FC * i + c + 1)
                        wait(act, ph.h_lo, FC * (i - 1) + c + 1)
                        a.activation(h_sb[:, c, :], bank[c][:, :], ACT.Gelu_apprx_tanh, bias=b1_of(i, c))\
                            .then_inc(ph.gelu, 1)
                if runs(i, 1, tiles):
                    k = i - 1
                    act.wait_ge(ph.down, FC * i)
                    wait(act, ph.tout, k - 1)
                    a.activation(yt[1 - par], bank[DOWN][:, :], ACT.Identity, bias=b2_of(k)).then_inc(ph.yt, 1)
                if ph is ex and runs(i, 2, tiles):
                    k = i - 2
                    act.wait_ge(ph.tout, k + 1)
                    wait(act, ph.y_out[par], (half - 1) * 16 * SJ)
                    a.activation(y_sb[par], bank[TOUT][:, :].rearrange("p (j d) -> p j d", j=SJ), ACT.Copy)\
                        .then_inc(ph.y, 1)

            pipeline(act, SH_TILES, 0, 2, lambda act, i, par, half: ffn_act(
                act, i, par, half, sh, SH_TILES, lambda i, c: sb1_sb[:, c:c + 1], lambda k: sb2_sb[:, 0:1]))
            act.wait_ge(tables, 1)
            pipeline(act, SLOT_TILES, 1, 2, lambda act, i, par, half: ffn_act(
                act, i, par, half, ex, SLOT_TILES,
                lambda i, c: b_tile[:, bass.ds(i, 1), c:c + 1].rearrange("p a b -> p (a b)"),
                lambda k: b_tile[:, bass.ds(k, 1), FC:FC + 1].rearrange("p a b -> p (a b)")))

        @block.vector
        def _(dve):
            v = nc.vector
            link = chain(dve, dve_step)

            def stats(b, buf, out_mv, done):
                for t in range(TB):
                    last = v.bn_stats(buf[:, t, :], x_all[:, b * TB + t, :])
                link(last)
                for t in range(TB):
                    last = v.bn_aggr(out_mv[:, t, :], buf[:, t, :])
                if done is None:
                    link(last)
                else:
                    last.then_inc(done, 1)
                    dve.wait_ge(done, b + 1)

            def stats1_batch(b):
                dve.wait_ge(x_in[b], 16)
                stats(b, st, mv[:, b * TB:(b + 1) * TB, :], stat1)

            def shift1(b):
                cols = slice(b * TB, (b + 1) * TB)
                dve.wait_ge(pow1, b + 1)
                v.scalar_tensor_tensor(shift[:, cols], mv[:, cols, 0], -1.0, rstd[:, cols], ALU.mult, ALU.mult)\
                    .then_inc(shift1_done, 1)

            stats1_batch(0)
            shift1(0)
            for b in range(1, BATCHES):
                stats1_batch(b)
            dve.wait_ge(comb_ready, 1)
            link(v.tensor_tensor(bcomb[:, :], bank[1][:, 0:3], bqkv_sb[:, :], ALU.add))
            v.tensor_scalar(bcomb[:, 0:1], bcomb[:, 0:1], SCALE, None, ALU.mult).then_inc(comb_b, 1)
            link(v.tensor_copy(rw_hi[:, :], rw_sb[:, :]))
            v.tensor_tensor(rw_lo[:, :], rw_sb[:, :], rw_hi[:, :].bitcast(fp32), ALU.subtract).then_inc(rw_split, 1)
            dve.wait_ge(const_ready, 1)
            for b in range(1, BATCHES):
                shift1(b)

            def softmax(c):
                dve.wait_ge(scores, c + 1)
                wait(dve, probs_lo, c)
                s = bank[2][:, 0:NEIGH * GT].rearrange("p (n t) -> p n t", n=NEIGH)
                link(v.tensor_reduce(top[:, :], s.rearrange("p n t -> p t n"), X, ALU.max))
                v.tensor_tensor(soft[:, :, :], s, top[:, :].unsqueeze(1).to_broadcast([P, NEIGH, GT]),
                                ALU.subtract).then_inc(shifted, 1)
                dve.wait_ge(exps, c + 1)
                link(v.tensor_reduce(inv[:, :], soft[:, :, :].rearrange("p n t -> p t n"), X, ALU.add))
                link(v.reciprocal(inv[:, :], inv[:, :]))
                v.tensor_tensor(soft[:, :, :], soft[:, :, :], inv[:, :].unsqueeze(1).to_broadcast([P, NEIGH, GT]),
                                ALU.mult).then_inc(probs, 1)
                dve.wait_ge(probs_hi, c + 1)
                v.tensor_tensor(p_lo[:, :, :], soft[:, :, :], p_hi[:, :, :].bitcast(fp32), ALU.subtract)\
                    .then_inc(probs_lo, 1)

            def products(b):
                dve.wait_ge(proj_out, 8 * b + 8)
                dve.wait_ge(halo, b + 1)
                wait(dve, scores, b)
                for n in range(NEIGH):
                    v.tensor_tensor(prod[:, n, :], q_sb, k_sb[:, n:n + SEQ], ALU.mult).then_inc(prod_done, 1)

            def weigh(c, half):
                for n in range(NEIGH):
                    use = (2 * c + half) * NEIGH + n
                    dve.wait_ge(spread, use + 1)
                    wait(dve, y_ready, 2 * c + half)
                    v.tensor_tensor(weighted[:, n, :], bank[3 + use % 2][:, :],
                                    v_sb[c % 2][:, n + half * 512:n + (half + 1) * 512], ALU.mult)\
                        .then_inc(weighted_v, 1)

            def residual(c):
                dve.wait_ge(bo_added, c + 1)
                for j in range(2):
                    dve.wait_ge(y_ready, 2 * c + j + 1)
                    part = x_all[:, c * TB + 4 * j:c * TB + 4 * j + 4, :]
                    v.tensor_tensor(part, bank[5 + j][:, :].rearrange("p (t d) -> p t d", d=D), part, ALU.add)\
                        .then_inc(resid, 1)
                dve.wait_ge(resid, 2 * (c + 1))
                wait(dve, norm2, c)
                stats(c, st2, mv2, None)
                v.tensor_scalar(rstd2[:, :], mv2[:, :, 1], EPS, None, ALU.add).then_inc(var2, 1)
                dve.wait_ge(rough2, c + 1)
                link(v.tensor_tensor(rstd2[:, :], rstd2[:, :], newton[:, :], ALU.mult))
                link(v.tensor_tensor(rstd2[:, :], rstd2[:, :], newton[:, :], ALU.mult))
                link(v.tensor_scalar(rstd2[:, :], rstd2[:, :], -0.5, 1.5, ALU.mult, ALU.add))
                link(v.tensor_tensor(rstd2[:, :], rstd2[:, :], newton[:, :], ALU.mult))
                v.scalar_tensor_tensor(shift2[:, :], mv2[:, :, 0], -1.0, rstd2[:, :], ALU.mult, ALU.mult)\
                    .then_inc(shift2_done, 1)

            def transposed2(c):
                for j in range(2):
                    dve.wait_ge(xt_hi_done, 2 * c + j + 1)
                    cols = slice(c * SEQ + j * 512, c * SEQ + (j + 1) * 512)
                    v.tensor_tensor(xt_lo[:, cols], bank[5 + j][:, :], xt_hi[:, cols].bitcast(fp32), ALU.subtract)\
                        .then_inc(xt_lo_done, 1)

            over = lambda m: m[:, :].unsqueeze(2).to_broadcast([P, TB, EXPERTS])
            by_expert = lambda m: m[:, :].unsqueeze(1).to_broadcast([P, TB, EXPERTS])

            def choose(c):
                dve.wait_ge(logits, c + 1)
                link(v.tensor_tensor(lg[:, :, :], bank[7][:, 0:TB * EXPERTS].rearrange("p (t e) -> p t e", e=EXPERTS),
                                     by_expert(rb_bc), ALU.add))
                for best, sel in ((m1, sel1), (m2, sel2)):
                    link(v.tensor_reduce(best[:, :], lg[:, :, :], X, ALU.max))
                    link(v.tensor_tensor(cand[:, :, :], lg[:, :, :], over(best), ALU.is_ge))
                    link(v.tensor_tensor(cand[:, :, :], cand[:, :, :], by_expert(rank_weight), ALU.mult))
                    link(v.tensor_reduce(km[:, :], cand[:, :, :], X, ALU.max))
                    link(v.tensor_tensor(sel[:, :, :], cand[:, :, :], over(km), ALU.is_equal))
                    if sel is sel1:
                        if c >= 2:
                            dve.wait_ge(scattered[c - 2], 16 * 2 * TB)
                        link(v.tensor_scalar(rows[c % 2][:, :, D + 1], km[:, :], -1.0, float(EXPERTS), ALU.mult, ALU.add))
                        link(v.scalar_tensor_tensor(lg[:, :, :], sel1[:, :, :], -3.0e38, lg[:, :, :], ALU.mult, ALU.add))
                v.tensor_tensor(either[:, :, :], sel1[:, :, :], sel2[:, :, :], ALU.add).then_inc(chosen, 1)
                v.tensor_tensor(gap[:, :], m2[:, :], m1[:, :], ALU.subtract).then_inc(gap_ready, 1)

            def place(c):
                tiles = slice(c * TB, (c + 1) * TB)
                dve.wait_ge(gap_exp, c + 1)
                link(v.tensor_scalar(gate2[:, tiles], eg[:, :], 1.0, None, ALU.add))
                link(v.reciprocal(gate1[:, tiles], gate2[:, tiles]))
                link(v.tensor_tensor(gate2[:, tiles], gate1[:, tiles], eg[:, :], ALU.mult))
                dve.wait_ge(ranks, c + 1)
                link(v.tensor_tensor(slot_at[:, :, :], bank[7][:, 64:64 + TB * EXPERTS].rearrange("p (t e) -> p t e", e=EXPERTS),
                                     by_expert(base), ALU.add))
                link(v.tensor_tensor(base[:, :], bank[7][:, 128:128 + EXPERTS], base[:, :], ALU.add))
                link(v.tensor_tensor(sel1[:, :, :], sel1[:, :, :], slot_at[:, :, :], ALU.mult))
                link(v.tensor_tensor(sel2[:, :, :], sel2[:, :, :], slot_at[:, :, :], ALU.mult))
                with nc.allow_low_precision(reason="row numbers are small integers"):
                    link(v.tensor_reduce(pos1[:, tiles], sel1[:, :, :], X, ALU.add))
                    v.tensor_reduce(pos2[:, tiles], sel2[:, :, :], X, ALU.add).then_inc(routed, 1)
                dve.wait_ge(routed, c + 1)

            for b in range(BATCHES + 2):
                if 1 <= b <= BATCHES:
                    softmax(b - 1)
                if b >= 2:
                    transposed2(b - 2)
                if b < BATCHES:
                    products(b)
                if 1 <= b <= BATCHES:
                    weigh(b - 1, 0)
                if b >= 2:
                    choose(b - 2)
                if 1 <= b <= BATCHES:
                    weigh(b - 1, 1)
                    residual(b - 1)
                if b >= 2:
                    place(b - 2)

            link(v.tensor_copy(pad_at[:, :], base[:, :]))
            link(v.tensor_tensor(n_tiles[:, :], base[:, :], region_start[:, :], ALU.subtract))
            link(v.tensor_scalar(n_int[:, :], n_tiles[:, :], float(SLOT - 1), None, ALU.add))
            link(v.tensor_single_scalar(n_int[:, :], n_int[:, :], SLOT.bit_length() - 1, ALU.arith_shift_right))
            link(v.tensor_copy(n_tiles[:, :], n_int[:, :]))
            link(v.tensor_copy(ends[:, 0, 4:], n_int[:, :]))
            for k in range(3):
                link(v.tensor_tensor(ends[:, k + 1, 4:], ends[:, k, 4:], ends[:, k, 4 - (1 << k):4 + EXPERTS - (1 << k)],
                                     ALU.add))
            full = [P, SLOT_TILES, EXPERTS]
            link(v.tensor_tensor(passed, slot_no[:, :].unsqueeze(2).to_broadcast(full),
                                 ends[:, 3, 4:].unsqueeze(1).to_broadcast(full), ALU.is_ge))
            link(v.tensor_reduce(slot_expert[:, :], passed, X, ALU.add))
            link(v.tensor_tensor(passed_n, passed, n_tiles[:, :].unsqueeze(1).to_broadcast(full), ALU.mult))
            link(v.tensor_reduce(n_passed[:, :], passed_n, X, ALU.add))
            link(v.tensor_tensor(n_passed[:, :], slot_no[:, :], n_passed[:, :], ALU.subtract))
            link(v.tensor_scalar(row_of[:, :], slot_expert[:, :], float(REGION), None, ALU.mult))
            link(v.scalar_tensor_tensor(row_f[:, :], n_passed[:, :], float(SLOT), row_of[:, :], ALU.mult, ALU.add))
            link(v.tensor_scalar(slot_row[:, :], row_f[:, :], float(PAD_ROW), None, ALU.min))
            of = [P, SLOT_TILES, EXPERTS]
            dve.wait_ge(bias_in, 16 * 3)
            link(v.tensor_tensor(passed, region_start[:, :].unsqueeze(1).to_broadcast(of),
                                 row_of[:, :].unsqueeze(2).to_broadcast(of), ALU.is_equal))
            for part in range(FC + 1):
                link(v.tensor_tensor(passed_n, passed, b_all[:, :, part].unsqueeze(1).to_broadcast(of), ALU.mult))
                link(v.tensor_reduce(b_tile[:, :, part], passed_n, X, ALU.add))
            v.tensor_scalar(slot_w[:, :], slot_expert[:, :], float(EXPERTS - 1), None, ALU.min).then_inc(tables, 1)

            def ffn_dve(dve, i, par, half, ph, tiles):
                if ph is ex and runs(i, -1, tiles):
                    k, kpar = i + 1, 1 - par
                    dve.wait_ge(ph.rows_in[kpar], (half + par + 1) * 16)
                    v.scalar_tensor_tensor(y_rows[:, bass.ds(k * SJ, SJ)], xs[kpar][:, :, D + 1],
                                           slot_expert[:, bass.ds(k, 1)], xs[kpar][:, :, D],
                                           ALU.is_equal, ALU.add).then_inc(ph.idx, 1)
                    dve.wait_ge(ph.xs_hi, k + 1)
                    v.tensor_tensor(xs_lo[kpar], bank[TIN][:, :], xs_hi[kpar].bitcast(fp32),
                                    ALU.subtract).then_inc(ph.xs_lo, 1)
                if runs(i, 0, tiles):
                    for c in range(FC):
                        dve.wait_ge(ph.gelu, FC * i + c + 1)
                        wait(dve, ph.down, FC * (i - 1) + c + 1)
                        v.tensor_copy(h_hi[:, c, :], h_sb[:, c, :]).then_inc(ph.h_hi, 1)
                        dve.wait_ge(ph.h_hi, FC * i + c + 1)
                        v.tensor_tensor(h_lo[:, c, :], h_sb[:, c, :], h_hi[:, c, :].bitcast(fp32),
                                        ALU.subtract).then_inc(ph.h_lo, 1)
                if ph is sh and runs(i, 2, tiles):
                    k = i - 2
                    dve.wait_ge(ph.tout, k + 1)
                    part = x_all[:, bass.ds(k * SJ, SJ), :]
                    v.tensor_tensor(part, bank[TOUT][:, :].rearrange("p (j d) -> p j d", j=SJ), part,
                                    ALU.add).then_inc(ph.y, 1)

            pipeline(dve, SH_TILES, 0, 2, lambda dve, i, par, half: ffn_dve(dve, i, par, half, sh, SH_TILES))
            pipeline(dve, SLOT_TILES, 1, 2, lambda dve, i, par, half: ffn_dve(dve, i, par, half, ex, SLOT_TILES))

            dve.wait_ge(sh.y, SH_TILES)
            for g in range(TILES // 4):
                dve.wait_ge(y_in[g % 2], 16 * (g // 2 + 1))
                for k, gate in enumerate((gate2, gate1)):
                    for t in range(4):
                        tile = g * 4 + t
                        ins = v.scalar_tensor_tensor(x_all[:, tile, :], y_back[g % 2][:, t, k * D:(k + 1) * D], gate[:, tile:tile + 1],
                                                     x_all[:, tile, :], ALU.mult, ALU.add)
                    if k == 0:
                        link(ins)
                ins.then_inc(summed, 1)

        @block.tensor
        def _(pe):
            m = nc.tensor
            pe.wait_ge(w_in, W_LOADS)
            m.matmul(bank[0][:, 0:3 * D], wp_sb[:, :], wqkv_sb[:, :], start=True, stop=True)
            for i in range(3):
                last = m.matmul(bank[1][:, i:i + 1], wqkv_sb[:, i * D:(i + 1) * D], bp_sb[:, :], start=True, stop=True)
            last.then_inc(comb_ready, 1)
            pe.wait_ge(comb_w, 1)
            pe.wait_ge(comb_b, 1)

            def project(b, uses):
                for j in uses:
                    use = 8 * b + j
                    wait(pe, proj_out, use - 1)
                    to = bank[use % 2]
                    if j < 2:
                        pe.wait_ge(norm1, b + 1)
                        for t in range(4):
                            last = m.transpose(to[:, t * D:(t + 1) * D], xn[:, 4 * j + t, :], ident[:, :])
                    else:
                        if j == 2:
                            pe.wait_ge(proj_out, 8 * b + 2)
                        w = (j - 2) // 2
                        last = m.matmul(to[:, :], wcomb[:, w * D:(w + 1) * D], xnt[:, (j % 2) * 512:(j % 2 + 1) * 512],
                                        start=True, stop=True)
                    last.then_inc(proj_ready, 1)

            def score(b):
                pe.wait_ge(prod_done, NEIGH * (b + 1))
                wait(pe, shifted, b)
                for n in range(NEIGH):
                    for grp in range(GROUPS):
                        off = P - HEADS - HEADS * grp
                        last = m.matmul(bank[2][:, n * GT:(n + 1) * GT], score_mask[:, off:off + P],
                                        prod[:, n, grp * GT:(grp + 1) * GT], start=(grp == 0), stop=(grp == GROUPS - 1))
                last.then_inc(scores, 1)

            def spread_probs(c, half):
                pe.wait_ge(probs_lo, c + 1)
                for n in range(NEIGH):
                    use = (2 * c + half) * NEIGH + n
                    wait(pe, weighted_v, use - 1)
                    for k in range(4):
                        to = bank[3 + use % 2][:, k * GT:(k + 1) * GT]
                        mask = expand[:, 4 * half + k, :]
                        m.matmul(to, mask, p_hi[:, n, :], start=True, stop=False)
                        last = m.matmul(to, mask, p_lo[:, n, :], start=False, stop=True)
                    last.then_inc(spread, 1)

            def out_project(c, half):
                pe.wait_ge(weighted_v, (2 * c + half + 1) * NEIGH)
                wait(pe, xt_lo_done, 2 * (c - 1) + half + 1 if c else 0)
                for t in range(4):
                    for n in range(NEIGH):
                        last = m.matmul(bank[5 + half][:, t * D:(t + 1) * D], weighted[:, n, t * P:(t + 1) * P],
                                        wo_sb[:, :], start=(n == 0), stop=(n == NEIGH - 1))
                last.then_inc(y_ready, 1)

            def transpose2(c):
                pe.wait_ge(norm2, c + 1)
                pe.wait_ge(resid, 2 * (c + 1))
                for j in range(2):
                    for t in range(4):
                        last = m.transpose(bank[5 + j][:, t * D:(t + 1) * D], rows[c % 2][:, 4 * j + t, 0:D], ident[:, :])
                    last.then_inc(t2_ready, 1)

            def router(c):
                pe.wait_ge(xt_lo_done, 2 * (c + 1))
                pe.wait_ge(rw_split, 1)
                wait(pe, routed, c)
                for t in range(TB):
                    cols = slice((c * TB + t) * P, (c * TB + t + 1) * P)
                    to = bank[7][:, t * EXPERTS:(t + 1) * EXPERTS]
                    m.matmul(to, xt_hi[:, cols], rw_hi[:, :], start=True, stop=False)
                    m.matmul(to, xt_hi[:, cols], rw_lo[:, :], start=False, stop=False)
                    last = m.matmul(to, xt_lo[:, cols], rw_hi[:, :], start=False, stop=True)
                last.then_inc(logits, 1)

            def rank(c):
                pe.wait_ge(chosen, c + 1)
                to = bank[7][:, 64:64 + TB * EXPERTS].rearrange("p (t e) -> p t e", e=EXPERTS)
                m.matmul(to, before[:, :], either[:, :, :], start=True, stop=False, skip_group_check=True)
                for back in range(1, TB):
                    m.matmul(to[:, back:, :], ones_bf[:, :], either[:, 0:TB - back, :], start=False,
                             stop=(back == TB - 1), skip_group_check=True)
                for t in range(TB):
                    last = m.matmul(bank[7][:, 128:128 + EXPERTS], ones_bf[:, :], either[:, t, :],
                                    start=(t == 0), stop=(t == TB - 1), skip_group_check=True)
                last.then_inc(ranks, 1)

            for b in range(BATCHES + 2):
                if b < BATCHES:
                    project(b, range(2))
                if b >= 2:
                    transpose2(b - 2)
                if b < BATCHES:
                    project(b, range(2, 8))
                if b >= 2:
                    router(b - 2)
                if 1 <= b <= BATCHES:
                    for half in range(2):
                        spread_probs(b - 1, half)
                        out_project(b - 1, half)
                if b >= 2:
                    rank(b - 2)
                if b < BATCHES:
                    score(b)

            def ffn_pe(pe, i, par, half, ph, tiles, w_of, hi_of, lo_of):
                if ph is ex and runs(i, -1, tiles):
                    k, kpar = i + 1, 1 - par
                    pe.wait_ge(ph.rows_in[kpar], (half + par + 1) * 16)
                    wait(pe, ph.xs_lo, k)
                    for j in range(SJ):
                        last = m.transpose(bank[TIN][:, j * P:(j + 1) * P], xs[kpar][:, j, 0:D], ident[:, :])
                    last.then_inc(ph.tin, 1)
                if runs(i, 0, tiles):
                    w = w_of(par)
                    if ph is ex:
                        pe.wait_ge(ph.w_in[0][par], (half + 1) * 16)
                        pe.wait_ge(ph.xs_lo, i + 1)
                    hi, lo = hi_of(i, par), lo_of(i, par)
                    for c in range(FC):
                        wait(pe, ph.gelu, FC * (i - 1) + c + 1)
                        w_hi, w_lo = w[:, 0, c * P:(c + 1) * P], w[:, 1, c * P:(c + 1) * P]
                        m.matmul(bank[c][:, :], w_hi, hi, start=True, stop=False)
                        m.matmul(bank[c][:, :], w_hi, lo, start=False, stop=False)
                        m.matmul(bank[c][:, :], w_lo, hi, start=False, stop=True).then_inc(ph.up, 1)
                if runs(i, 2, tiles):
                    pe.wait_ge(ph.yt, i - 1)
                    wait(pe, ph.y, i - 2)
                    for j in range(SJ):
                        last = m.transpose(bank[TOUT][:, j * P:(j + 1) * P], yt[par][:, j * P:(j + 1) * P], ident[:, :])
                    last.then_inc(ph.tout, 1)
                if runs(i, 1, tiles):
                    k = i - 1
                    w = w_of(1 - par)
                    if ph is ex:
                        pe.wait_ge(ph.w_in[1][1 - par], (half + par) * 16)
                    wait(pe, ph.yt, k)
                    for c in range(FC):
                        pe.wait_ge(ph.h_lo, FC * k + c + 1)
                        w_hi, w_lo = w[:, 2, c * P:(c + 1) * P], w[:, 3, c * P:(c + 1) * P]
                        m.matmul(bank[DOWN][:, :], w_hi, h_hi[:, c, :], start=(c == 0), stop=False)
                        m.matmul(bank[DOWN][:, :], w_hi, h_lo[:, c, :], start=False, stop=False)
                        m.matmul(bank[DOWN][:, :], w_lo, h_hi[:, c, :], start=False, stop=(c == FC - 1))\
                            .then_inc(ph.down, 1)

            pe.wait_ge(raw_hi, 2)
            pe.wait_ge(raw_lo, 2)
            pe.wait_ge(routed, BATCHES)
            pipeline(pe, SH_TILES, 0, 2, lambda pe, i, par, half: ffn_pe(
                pe, i, par, half, sh, SH_TILES, lambda par: sw,
                lambda i, par: xt_hi[:, bass.ds(i * SLOT, SLOT)], lambda i, par: xt_lo[:, bass.ds(i * SLOT, SLOT)]))
            pipeline(pe, SLOT_TILES, 1, 2, lambda pe, i, par, half: ffn_pe(
                pe, i, par, half, ex, SLOT_TILES, lambda par: stage[par],
                lambda i, par: xs_hi[par], lambda i, par: xs_lo[par]))

    return nc


def kernel(**inputs):
    import numpy as np
    import concourse.bacc as bacc
    from concourse.bass_utils import run_bass_kernel_spmd

    p = {k.replace("L0_", ""): np.asarray(v) for k, v in inputs.items()}
    t = lambda a: np.ascontiguousarray(np.swapaxes(a, -1, -2))
    chunks = lambda a: np.ascontiguousarray(a.reshape(a.shape[:-1] + (-1, P)).swapaxes(-1, -2))
    arrays = {
        "x": p["attn_x"],
        "wp": p["attn_Wp"],
        "bp": p["attn_bp"],
        "wqkv_t": np.concatenate([t(p["attn_Wq"]), t(p["attn_Wk"]), t(p["attn_Wv"])], axis=1),
        "bqkv": t(np.stack([p["attn_bq"], p["attn_bk"], p["attn_bv"]])),
        "wo_t": t(p["attn_Wo"]),
        "bo": p["attn_bo"],
        "sw1_t": t(p["ffn_shared_w1"]),
        "sb1": chunks(p["ffn_shared_b1"]),
        "sw2_t": t(p["ffn_shared_w2"]),
        "sb2": p["ffn_shared_b2"],
        "rw_t": t(p["ffn_router_w"]),
        "rb": p["ffn_router_b"],
        "ew1_t": t(p["ffn_spec_w1"]),
        "ew2_t": t(p["ffn_spec_w2"]),
        "eb": np.concatenate([chunks(p["ffn_spec_b1"]).swapaxes(0, 1), t(p["ffn_spec_b2"])[:, :, None]], axis=2),
    }
    nc = bacc.Bacc("TRN2", target_bir_lowering=False, num_devices=1)
    args = {}
    for name, a in arrays.items():
        arrays[name] = a = np.ascontiguousarray(a)
        args[name] = nc.dram_tensor(name, a.shape, mybir.dt.from_np(a.dtype), kind="ExternalInput").ap()
    out = nc.dram_tensor("out", (BATCHES, SEQ, D), mybir.dt.float32, kind="ExternalOutput").ap()
    preln_local_attention_moe(nc, **args, out=out)
    r = run_bass_kernel_spmd(nc, [arrays], core_ids=[0])
    return r.results[0]["out"]
```

```python
import concourse.bass as bass
from concourse import mybir
from contextlib import ExitStack

P = 128
BATCHES, SEQ, D = 4, 1024, 128
TOKENS = BATCHES * SEQ
HEADS = 16
HEAD_DIM = D // HEADS
NEIGH = 3
FF = 512
FC = FF // P
EXPERTS = 8
EPS = 1e-5

TB = SEQ // P
TILES = TOKENS // P
GROUPS = P // HEADS
GT = SEQ // GROUPS

SLOT = 512
SJ = SLOT // P
REGION = TOKENS + SLOT
PAD_ROW = EXPERTS * REGION
XG_ROWS = PAD_ROW + SLOT
ROW = D + 2
SLOT_TILES = 2 * TOKENS // SLOT + EXPERTS - 1
PAD_TOKEN = 4 * TOKENS
SH_TILES = TOKENS // SLOT


def preln_local_attention_moe(nc, x, attn_w, bo, sw1_t, sb1, sw2_t, sb2, rb,
                              ew1_t, ew2_t, eb, out):
    fp32, fp32r = mybir.dt.float32, mybir.dt.float32r
    bf16, int32 = mybir.dt.bfloat16, mybir.dt.int32
    ALU = mybir.AluOpType
    ACT = mybir.ActivationFunctionType
    X = mybir.AxisListType.X
    SCALE = float(HEAD_DIM) ** -0.5

    xg = nc.dram_tensor("rows_by_expert", (XG_ROWS, ROW), fp32, kind="Internal").ap()
    yg = nc.dram_tensor("expert_outputs", (2 * TOKENS, D), fp32, kind="Internal").ap()

    with ExitStack() as ctx:
        def sb(name, shape, dt=fp32):
            return ctx.enter_context(nc.sbuf_tensor(name, shape, dt))

        def sem(name):
            return ctx.enter_context(nc.semaphore(name))

        bank = [ctx.enter_context(nc.psum_tensor(f"bank{i}", [P, 512], fp32)) for i in range(8)]

        ident = sb("ident", [P, P])
        score_mask = sb("score_mask", [P, 2 * P - HEADS])
        expand = sb("expand", [P, GROUPS, P], fp32r)
        before = sb("before", [P, P], bf16)
        ones_bf = sb("ones_bf", [P, P], bf16)
        rank_weight = sb("rank_weight", [P, EXPERTS])
        region_start = sb("region_start", [P, EXPERTS])
        half_neg = sb("half_neg", [P, TILES])
        one = sb("one", [P, 1])
        gap = sb("gap", [P, TILES])
        slot_no = sb("slot_no", [P, SLOT_TILES])

        attn_sb = sb("attn_sb", [P, 5 * D + EXPERTS + 4])
        at = [0]

        def part_of(n):
            at[0] += n
            return attn_sb[:, at[0] - n:at[0]]

        wp_sb, wqkv_sb, wo_sb, rw_sb = part_of(D), part_of(3 * D), part_of(D), part_of(EXPERTS)
        bp_sb, bqkv_sb = part_of(1), part_of(3)
        wcomb = sb("wcomb", [P, 3 * D])
        bcomb = sb("bcomb", [P, 3])
        bo_bc = sb("bo_bc", [P, D])
        rw_parts = sb("rw_parts", [P, 2, EXPERTS], fp32r)
        rb_bc = sb("rb_bc", [P, EXPERTS])

        x_all = sb("x_all", [P, TILES, D])
        rows = [sb(f"rows{i}", [P, TB, ROW]) for i in range(2)]
        xt_hi = sb("xt_hi", [P, TOKENS], fp32r)
        xt_lo = sb("xt_lo", [P, TOKENS], fp32r)
        gate1 = sb("gate1", [P, TILES])
        gate2 = sb("gate2", [P, TILES])
        pos1 = sb("pos1", [P, TILES], int32)
        pos2 = sb("pos2", [P, TILES], int32)

        w_all = sb("w_all", [P, EXPERTS, 4, FF], fp32r)
        b_all = sb("b_all", [P, EXPERTS, FC + 1])
        b_tile = sb("b_tile", [P, SLOT_TILES, FC + 1])
        sb1_sb = sb("sb1_sb", [P, FC])
        sb2_sb = sb("sb2_sb", [P, 1])

        raw = [sb(f"raw{i}", [P, FF]) for i in range(2)]
        sw = sb("sw", [P, 4, FF], fp32r)
        h_hi = sb("h_hi", [P, FC, SLOT], fp32r)
        h_lo = sb("h_lo", [P, FC, SLOT], fp32r)
        stage = [xt[:, SEQ:SEQ + 4 * FF].rearrange("p (w f) -> p w f", w=4) for xt in (xt_hi, xt_lo)]
        xs_hi = [xt[:, SEQ + 4 * FF:SEQ + 4 * FF + SLOT] for xt in (xt_hi, xt_lo)]
        xs_lo = [xt[:, SEQ + 4 * FF + SLOT:SEQ + 4 * FF + 2 * SLOT] for xt in (xt_hi, xt_lo)]

        ARENA = 2 * SEQ + NEIGH * 512 + 3 * (SEQ + 2) + NEIGH * SEQ
        arena = sb("arena", [P, ARENA])
        at = [0]

        def piece(n):
            at[0] += n
            assert at[0] <= ARENA
            return arena[:, at[0] - n:at[0]]

        xn = piece(TB * D).rearrange("p (t d) -> p t d", d=D)
        xnt = piece(SEQ)
        piece(NEIGH * 512 - SEQ)
        weighted = arena[:, TB * D:TB * D + NEIGH * 512].rearrange("p (n t) -> p n t", n=NEIGH)
        q_sb = piece(SEQ)
        k_sb = piece(SEQ + 2)
        v_sb = [piece(SEQ + 2) for _ in range(2)]
        prod = piece(NEIGH * SEQ).rearrange("p (n t) -> p n t", n=NEIGH)
        prod_as_weighted = arena[:, at[0] - NEIGH * SEQ:at[0] - NEIGH * SEQ + NEIGH * 512].rearrange(
            "p (n t) -> p n t", n=NEIGH)
        expand_raw = prod[:, 0, :]
        at[0] = 0
        h_sb = piece(FC * SLOT).rearrange("p (c t) -> p c t", c=FC)
        yt = [piece(SLOT) for _ in range(2)]
        y_sb = [piece(SLOT).rearrange("p (j d) -> p j d", j=SJ) for _ in range(2)]
        xs = [piece(SJ * ROW).rearrange("p (j d) -> p j d", j=SJ) for _ in range(2)]
        pad_rows = piece(SJ * ROW).rearrange("p (j d) -> p j d", j=SJ)
        passed = piece(SLOT_TILES * EXPERTS).rearrange("p (s e) -> p s e", e=EXPERTS)
        b_of = piece(SLOT_TILES * (FC + 1) * EXPERTS).rearrange("p (s f e) -> p s f e", e=EXPERTS, f=FC + 1)
        passed_n = piece(SLOT_TILES * EXPERTS).rearrange("p (s e) -> p s e", e=EXPERTS)
        at[0] = FC * SLOT + 2 * SLOT
        Y_GROUPS = TILES // 4
        y_back = [piece(2 * 4 * D) for _ in range(Y_GROUPS - 2)] + [
            r[:, :, :].rearrange("p t c -> p (t c)")[:, 0:2 * 4 * D] for r in rows]
        y_back = [y.rearrange("p (t kd) -> p t kd", t=4) for y in y_back]
        Y_ORDER = list(range(2, Y_GROUPS)) + [0, 1]

        warm = sb("warm", [P, 8])
        st = sb("st", [P, TB, 6])
        mv = sb("mv", [P, TILES, 2])
        rstd = sb("rstd", [P, TILES])
        shift = sb("shift", [P, TILES])
        st2 = sb("st2", [P, TB, 6])
        mv2 = sb("mv2", [P, TB, 2])
        rstd2 = sb("rstd2", [P, TB])
        neg_half = sb("neg_half", [P, TB])
        guess = sb("guess", [P, TB], int32)
        square = sb("square", [P, TB])
        top = sb("top", [P, GT])
        soft = sb("soft", [P, NEIGH, GT])
        p_hi = sb("p_hi", [P, NEIGH, GT], fp32r)
        p_lo = sb("p_lo", [P, NEIGH, GT], fp32r)
        inv = sb("inv", [P, GT])

        lg = sb("lg", [P, TB, EXPERTS])
        cand = sb("cand", [P, TB, EXPERTS])
        sel1 = sb("sel1", [P, TB, EXPERTS])
        sel2 = sb("sel2", [P, TB, EXPERTS])
        either = sb("either", [P, TB, EXPERTS], bf16)
        m1 = sb("m1", [P, TB])
        m2 = sb("m2", [P, TB])
        km = sb("km", [P, TB])
        slot_at = sb("slot_at", [P, TB, EXPERTS])
        base = sb("base", [P, EXPERTS])

        n_int = sb("n_int", [P, EXPERTS], int32)
        n_tiles = sb("n_tiles", [P, EXPERTS])
        ends = sb("ends", [P, 4, 4 + EXPERTS])
        pad_at = sb("pad_at", [P, EXPERTS], int32)
        slot_expert = sb("slot_expert", [P, SLOT_TILES])
        n_passed = sb("n_passed", [P, SLOT_TILES])
        row_f = sb("row_f", [P, SLOT_TILES])
        row_of = sb("row_of", [P, SLOT_TILES])
        slot_row = sb("slot_row", [P, SLOT_TILES], int32)
        slot_w = sb("slot_w", [P, SLOT_TILES], int32)
        y_rows = sb("y_rows", [P, SJ * SLOT_TILES], int32)
        y_row = [sb(f"y_row{i}", [P, SJ], int32) for i in range(2)]

        TIN, DOWN, TOUT = 4, 5, 6
        SH_OUT = 7
        scores_at = bank[2][:, 0:NEIGH * GT]
        ranks_at = bank[2][:, NEIGH * GT:NEIGH * GT + TB * EXPERTS].rearrange("p (t e) -> p t e", e=EXPERTS)
        counts_at = bank[2][:, NEIGH * GT + TB * EXPERTS:NEIGH * GT + (TB + 1) * EXPERTS]
        logits_at = bank[2][:, NEIGH * GT:].rearrange("p (t i e) -> p t i e", i=2, e=EXPERTS)
        W_LOADS = 16 * 3
        out_view = lambda g: out.rearrange("b s d -> (b s) d")[g * 4 * P:(g + 1) * 4 * P, :].rearrange(
            "(t p) d -> p t d", p=P)

        x_in = [sem(f"x_in{b}") for b in range(BATCHES)]
        w_in = sem("w_in")
        bias_in = sem("bias_in")
        raw_in = [sem(f"raw_in{i}") for i in range(2)]
        raw_hi = sem("raw_hi")
        raw_lo = sem("raw_lo")
        const_ready = sem("const_ready")
        pool_step, dve_step = sem("pool_step"), sem("dve_step")
        comb_ready = sem("comb_ready")
        comb_w = sem("comb_w")
        comb_b = sem("comb_b")
        stat1, norm1 = sem("stat1"), sem("norm1")
        pow1, shift1_done = sem("pow1"), sem("shift1_done")
        bo_added = sem("bo_added")
        proj_ready = sem("proj_ready")
        proj_out = sem("proj_out")
        halo_k, halo_v = sem("halo_k"), sem("halo_v")
        prod_done = sem("prod_done")
        scores = sem("scores")
        shifted = sem("shifted")
        exps = sem("exps")
        probs, probs_hi, probs_lo = sem("probs"), sem("probs_hi"), sem("probs_lo")
        spread = sem("spread")
        weighted_v = sem("weighted_v")
        pad_ready = sem("pad_ready")
        y_ready = sem("y_ready")
        resid = sem("resid")
        norm2 = sem("norm2")
        t2_ready = sem("t2_ready")
        xt_hi_done, xt_lo_done = sem("xt_hi_done"), sem("xt_lo_done")
        rw_split = sem("rw_split")
        logits = sem("logits")
        chosen = sem("chosen")
        ranks = sem("ranks")
        gap_ready, gap_exp = sem("gap_ready"), sem("gap_exp")
        routed = sem("routed")
        scattered = [sem(f"scattered{c}") for c in range(BATCHES)]
        ends_known = sem("ends_known")
        tables = sem("tables")
        biases = sem("biases")
        gates, scaled = sem("gates"), sem("scaled")
        pad_out = sem("pad_out")
        y_in = [sem(f"y_in{i}") for i in range(TILES // 4)]
        second_in = sem("second_in")
        summed = sem("summed")
        out_done = sem("out_done")

        class Phase:
            def __init__(self, name):
                self.up = sem(f"{name}_up")
                self.gelu = sem(f"{name}_gelu")
                self.h_hi = sem(f"{name}_h_hi")
                self.h_lo = sem(f"{name}_h_lo")
                self.down = sem(f"{name}_down")
                self.yt = sem(f"{name}_yt")
                self.tout = sem(f"{name}_tout")
                self.y = sem(f"{name}_y")

        class SlotPhase(Phase):
            def __init__(self, name):
                super().__init__(name)
                self.rows_in = [sem(f"{name}_rows_in{i}") for i in range(2)]
                self.w_in = [[sem(f"{name}_w{layer}_in{i}") for i in range(2)] for layer in (1, 2)]
                self.tin = sem(f"{name}_tin")
                self.xs_hi = sem(f"{name}_xs_hi")
                self.xs_lo = sem(f"{name}_xs_lo")
                self.idx = sem(f"{name}_idx")
                self.row = sem(f"{name}_row")
                self.go = sem(f"{name}_go")
                self.y_out = [sem(f"{name}_y_out{i}") for i in range(2)]

        sh, ex = Phase("sh"), SlotPhase("ex")

        block = ctx.enter_context(nc.Block())

        def chain(eng, signal):
            n = [0]

            def link(ins):
                n[0] += 1
                ins.then_inc(signal, 1)
                eng.wait_ge(signal, n[0])
            return link

        def wait(eng, signal, value):
            if not isinstance(value, int) or value > 0:
                eng.wait_ge(signal, value)

        def steady(eng, first, last, step):
            assert first % 2 == 0 and (last - first) % 4 == 3
            with eng.Fori(0, (last - first + 1) // 4) as quad:
                for k in range(4):
                    step(eng, quad * 4 + (first + k), k % 2, quad * 2 + (first + k) // 2)

        def pipeline(eng, tiles, ahead, behind, step, done=0):
            first, last = behind + behind % 2 + 2, tiles - 1 - ahead
            last -= (last - first + 1) % 4
            for i in range(done - ahead, first):
                step(eng, i, i % 2, i // 2)
            steady(eng, first, last, step)
            for i in range(last + 1, tiles + behind):
                step(eng, i, i % 2, i // 2)

        def runs(i, back, tiles):
            return not isinstance(i, int) or 0 <= i - back < tiles

        ACT_HIGH = (1, 3)
        WEIGHT_PIECES = 2 * (EXPERTS + 1)
        POOL_PRODUCTS = 1
        DVE_PIECES = 5
        PIECES_AT = [3, 10] + [0] * BATCHES

        HALF_GROUPS = GROUPS // 2
        LAST = GROUPS * (BATCHES - 1)

        def neighbours_of(buf, first, n):
            at = buf[:, first:first + n]
            return bass.AP(tensor=at.tensor, offset=at.offset, ap=[list(at.ap[0]), [1, NEIGH], [1, n]])

        def spread_at(use):
            return bank[3 + use % 2] if use < LAST else bank[(3, 4, 0, 1)[(use - LAST) % 4]]

        def weighted_at(c, half):
            return weighted if c < BATCHES - 1 or half == 0 else prod_as_weighted

        SH_BATCH = SEQ // SLOT
        SH_BEFORE = SH_TILES - SH_BATCH
        SH_FIRST_LEFT = SH_BATCH
        SH_ROOMY = SH_FIRST_LEFT

        def shared_tiles(b):
            return range(SH_BATCH) if b == BATCHES - 1 else ()

        def sh_at(i):
            return (i + SH_BATCH) % SH_TILES

        def sh_bank(i, c):
            return bank[c % 2] if i < SH_ROOMY else bank[(0, 1, 3, 4)[c]]

        def sh_hidden(i, c):
            return raw[c % 2][:, :] if i < SH_ROOMY else h_sb[:, c, :]

        def sh_out(i):
            return bank[SH_OUT] if i < SH_ROOMY else bank[SH_OUT - i % 2]

        def sh_yt(i):
            return raw[0][:, :] if i < SH_ROOMY else yt[i % 2]

        def sh_chunk_before(i, c):
            return FC * i + c - (1 if i < SH_ROOMY else c if i == SH_ROOMY else 3)

        def raw_piece(n):
            if n < 2:
                src, dst = (sw1_t, sw2_t)[n], sw[:, :, :]
            else:
                e = n // 2 - 1
                src, dst = (ew1_t, ew2_t)[n % 2][e], w_all[:, e, :, :]
            return src, dst[:, 2 * (n % 2), :], dst[:, 2 * (n % 2) + 1, :]

        @block.sync
        def _(sp):
            for b in range(BATCHES):
                sp.dma_start(x_all[:, b * TB:(b + 1) * TB, :],
                             x[b].rearrange("(t p) d -> p t d", p=P)).then_inc(x_in[b], 16)
                if b == 0:
                    sp.wait_ge(x_in[0], 16)
            for n in range(WEIGHT_PIECES):
                wait(sp, raw_lo, n - 1)
                src = raw_piece(n)[0]
                if n % 2:
                    sp.dma_start(raw[n % 2][:, :].rearrange("p (c d) -> p c d", c=FC),
                                 src.rearrange("(c p) d -> p c d", p=P)).then_inc(raw_in[n % 2], 16)
                else:
                    sp.dma_start(raw[n % 2][:, :], src).then_inc(raw_in[n % 2], 16)

            sp.wait_ge(ends_known, 1)
            sp.wait_ge(pad_ready, 1)
            for e in range(EXPERTS):
                row = sp.value_load(pad_at[0:1, e:e + 1], min_val=e * REGION, max_val=e * REGION + TOKENS)
                sp.dma_start(xg[bass.ds(row, SLOT), :].rearrange("(j p) c -> p j c", p=P),
                             pad_rows).then_inc(pad_out, 16)
            sp.dma_start(xg[PAD_ROW:PAD_ROW + SLOT, :].rearrange("(j p) c -> p j c", p=P),
                         pad_rows).then_inc(pad_out, 16)
            sp.wait_ge(tables, 1)
            sp.wait_ge(raw_lo, WEIGHT_PIECES)
            sp.wait_ge(sh.up, FC * SH_BEFORE)

            def load_weights(sp, i, par, half, layer):
                k = i + 1
                if runs(i, -1, SLOT_TILES):
                    e = sp.value_load(slot_w[0:1, bass.ds(k, 1)], min_val=0, max_val=EXPERTS - 1)
                    wait(sp, (ex.up, ex.down)[layer], FC * (k - 1))
                    sp.dma_start(stage[1 - par][:, 2 * layer:2 * layer + 2, :].bitcast(fp32),
                                 w_all[:, bass.ds(e, 1), 2 * layer:2 * layer + 2, :]
                                 .rearrange("p a w f -> p (a w) f").bitcast(fp32))\
                        .then_inc(ex.w_in[layer][1 - par], 16)

            def load_rows(sp, i, par, half, before=None):
                k = i + 2
                if runs(i, -2, SLOT_TILES):
                    wait(sp, ex.tin, k - 1)
                    wait(sp, ex.idx, k - 1)
                    row = sp.value_load(slot_row[0:1, bass.ds(k, 1)], min_val=0, max_val=PAD_ROW)
                    if before is not None:
                        before()
                    sp.dma_start(xs[par], xg[bass.ds(row, SLOT), :].rearrange("(j p) c -> p j c", p=P))\
                        .then_inc(ex.rows_in[par], 16)

            def load_tile(sp, i, par, half):
                load_weights(sp, i, par, half, 0)
                load_rows(sp, i, par, half)
                load_weights(sp, i, par, half, 1)

            load_weights(sp, -1, 1, -1, 0)
            load_weights(sp, -1, 1, -1, 1)

            def rows_in_place():
                sp.wait_ge(pad_out, 16 * (EXPERTS + 1))
                for c in range(BATCHES):
                    sp.wait_ge(scattered[c], 16 * 2 * TB)

            load_rows(sp, -2, 0, -1, before=rows_in_place)
            load_rows(sp, -1, 1, -1)
            pipeline(sp, SLOT_TILES, 2, 0, load_tile, done=2)

            for par in range(2):
                sp.wait_ge(ex.y_out[par], 16 * SJ * ((SLOT_TILES + 1 - par) // 2))
            for g in Y_ORDER:
                sp.dma_start(y_back[g], yg[g * 8 * P:(g + 1) * 8 * P, :]
                             .rearrange("(t p k) d -> p t (k d)", p=P, k=2)).then_inc(y_in[g], 16)
            for n, g in enumerate(Y_ORDER):
                sp.wait_ge(summed, n + 1)
                sp.dma_start(out_view(g), x_all[:, g * 4:(g + 1) * 4, :]).then_inc(out_done, 16)
            sp.wait_ge(out_done, 16 * (TILES // 4))

        @block.gpsimd
        def _(pool):
            link = chain(pool, pool_step)
            g = nc.gpsimd
            link(g.memset(ident[:, :], 0.0))
            link(g.affine_select(out=ident[:, :], in_=ident[:, :], compare_op=ALU.not_equal, fill=1.0,
                                 base=0, pattern=[[-1, P]], channel_multiplier=1))
            link(g.memset(half_neg[:, :], -0.5))
            link(g.memset(one[:, :], 1.0))

            def add_bo(b):
                pool.wait_ge(norm1, b + 1)
                pool.wait_ge(w_in, W_LOADS)
                xb = x_all[:, b * TB:(b + 1) * TB, :]
                g.tensor_tensor(xb, xb, bo_bc[:, :].unsqueeze(1).to_broadcast([P, TB, D]), ALU.add)\
                    .then_inc(bo_added, 1)

            def split_weights(n):
                _, hi, lo = raw_piece(n)
                pool.wait_ge(raw_in[n % 2], 16 * (n // 2 + 1))
                pool.wait_ge(raw_lo, n)
                g.tensor_tensor(hi, raw[n % 2][:, :], one[:, :].to_broadcast([P, FF]), ALU.mult).then_inc(raw_hi, 1)
                pool.wait_ge(raw_hi, n + 1)
                g.tensor_tensor(lo, raw[n % 2][:, :], hi.bitcast(fp32), ALU.subtract).then_inc(raw_lo, 1)

            def scale1(b):
                cols = slice(b * TB, (b + 1) * TB)
                pool.wait_ge(stat1, b + 1)
                link(g.tensor_scalar_add(rstd[:, cols], mv[:, cols, 1], EPS))
                g.tensor_tensor(rstd[:, cols], rstd[:, cols], half_neg[:, cols], ALU.pow).then_inc(pow1, 1)

            def products(b):
                pool.wait_ge(proj_out, 8 * b + 6)
                pool.wait_ge(halo_k, b + 1)
                pool.wait_ge(scores, b)
                g.tensor_tensor(prod, q_sb.unsqueeze(1).to_broadcast([P, NEIGH, SEQ]), neighbours_of(k_sb, 0, SEQ),
                                ALU.mult).then_inc(prod_done, 1)

            scale1(0)
            link(g.memset(score_mask[:, :], 1.0))
            link(g.affine_select(out=score_mask[:, :], in_=score_mask[:, :], compare_op=ALU.is_ge, fill=0.0,
                                 base=HEAD_DIM * (P - HEADS), pattern=[[-HEAD_DIM, 2 * P - HEADS]],
                                 channel_multiplier=1))
            link(g.affine_select(out=score_mask[:, :], in_=score_mask[:, :], compare_op=ALU.is_ge, fill=0.0,
                                 base=HEAD_DIM - 1 - HEAD_DIM * (P - HEADS),
                                 pattern=[[HEAD_DIM, 2 * P - HEADS]], channel_multiplier=-1))
            link(g.memset(expand_raw[:, :], 0.0))
            link(g.affine_select(out=expand_raw[:, :], in_=expand_raw[:, :], compare_op=ALU.not_equal,
                                 fill=1.0, base=0, pattern=[[-HEADS, GROUPS], [-1, HEADS], [0, HEAD_DIM]],
                                 channel_multiplier=1))
            link(g.tensor_copy(expand[:, :, :].rearrange("p g d -> p (g d)"), expand_raw[:, :]))
            link(g.memset(ones_bf[:, :], 1.0))
            link(g.affine_select(out=before[:, :], in_=ones_bf[:, :], compare_op=ALU.is_gt, fill=0.0,
                                 base=0, pattern=[[1, P]], channel_multiplier=-1))
            link(g.iota(rank_weight[:, :], pattern=[[-1, EXPERTS]], base=EXPERTS, channel_multiplier=0,
                        allow_small_or_imprecise_dtypes=True))
            link(g.iota(region_start[:, :], pattern=[[REGION, EXPERTS]], base=0, channel_multiplier=0,
                        allow_small_or_imprecise_dtypes=True))
            link(g.tensor_copy(base[:, :], region_start[:, :]))
            link(g.iota(slot_no[:, :], pattern=[[1, SLOT_TILES]], base=0, channel_multiplier=0,
                        allow_small_or_imprecise_dtypes=True))
            g.memset(ends[:, :, :], 0.0).then_inc(const_ready, 1)
            for b in range(1, BATCHES):
                scale1(b)

            pieces = iter(range(DVE_PIECES, WEIGHT_PIECES))
            for b in range(BATCHES + 2):
                if b < BATCHES:
                    add_bo(b)
                if POOL_PRODUCTS <= b < BATCHES:
                    products(b)
                for _ in range(PIECES_AT[b]):
                    split_weights(next(pieces))
                if b >= 2:
                    c = b - 2
                    if c >= 2:
                        pool.wait_ge(scattered[c - 2], 16 * 2 * TB)
                    link(g.iota(rows[c % 2][:, :, D:D + 1], pattern=[[2 * P, TB], [0, 1]], base=2 * c * SEQ,
                                channel_multiplier=2, allow_small_or_imprecise_dtypes=True))
                    pool.wait_ge(norm2, c + 1)
                    pool.wait_ge(routed, c + 1)
                    if c == BATCHES - 1:
                        link(g.memset(pad_rows, 0.0))
                        link(g.memset(pad_rows[:, :, D:D + 1], float(PAD_TOKEN)))
                        g.memset(pad_rows[:, :, D + 1:D + 2], -1.0).then_inc(pad_ready, 1)
                    for t in range(TB):
                        for pos in (pos1, pos2):
                            g.indirect_dma_start(
                                xg[:, :], bass.IndirectOffsetOnAxis(ap=pos[:, c * TB + t:c * TB + t + 1], axis=0),
                                rows[c % 2][:, t, :], None).then_inc(scattered[c], 16)
            pool.wait_ge(tables, 1)

            last_row = pool.to_reg(2 * TOKENS - 1)

            def put_tile(pool, i, par, half):
                k = i - 2
                if runs(i, 2, SLOT_TILES):
                    wait(pool, ex.y_out[par], (half - 1) * 16 * SJ)
                    pool.wait_ge(ex.idx, k + 1)
                    g.tensor_copy(y_row[par][:, :], y_rows[:, bass.ds(k * SJ, SJ)]).then_inc(ex.row, 1)
                    pool.wait_ge(ex.row, k + 1)
                    pool.wait_ge(ex.y, k + 1)
                    pool.sem_inc(ex.go, 1)
                    for j in range(SJ):
                        g.indirect_dma_start(
                            yg[:, :], bass.IndirectOffsetOnAxis(ap=y_row[par][:, j:j + 1], axis=0),
                            y_sb[par][:, j, :], None, bounds_check=last_row, oob_is_err=False)\
                            .then_inc(ex.y_out[par], 16)
            pipeline(pool, SLOT_TILES, 0, 2, put_tile)

            for n, g4 in enumerate(Y_ORDER):
                pool.wait_ge(scaled, n + 1)
                pool.wait_ge(second_in, n + 1)
                part = x_all[:, g4 * 4:(g4 + 1) * 4, :]
                g.tensor_tensor(part, y_back[g4][:, :, D:2 * D], part, ALU.add).then_inc(summed, 1)

        @block.scalar
        def _(act):
            a = nc.scalar
            act.dma_start(attn_sb[:, :], attn_w).then_inc(w_in, 16)
            act.dma_start(bo_bc[:, :], bo.rearrange("(a n) -> a n", a=1).to_broadcast([P, D])).then_inc(w_in, 16)
            act.dma_start(rb_bc[:, :], rb.rearrange("(a n) -> a n", a=1).to_broadcast([P, EXPERTS])).then_inc(w_in, 16)
            act.dma_start(sb1_sb[:, :], sb1).then_inc(bias_in, 16)
            act.dma_start(sb2_sb[:, :], sb2.rearrange("(p a) -> p a", a=1)).then_inc(bias_in, 16)
            act.dma_start(b_all[:, :, :], eb).then_inc(bias_in, 16)

            def transposed2(act, a, c):
                if 0 <= c < BATCHES:
                    for j in range(2):
                        act.wait_ge(t2_ready, 2 * c + j + 1)
                        a.activation(xt_hi[:, c * SEQ + j * 512:c * SEQ + (j + 1) * 512], bank[5 + j][:, :],
                                     ACT.Copy).then_inc(xt_hi_done, 1)

            def probs_high(act, a, c):
                if 0 <= c < BATCHES:
                    act.wait_ge(probs, c + 1)
                    wait(act, spread, GROUPS * c)
                    a.activation(p_hi[:, :, :], soft[:, :, :], ACT.Copy).then_inc(probs_hi, 1)

            def norm(b, src_tile, r, sh, dst, done):
                for t in range(TB):
                    last = a.activation(dst[:, t, 0:D], x_all[:, b * TB + t, :], ACT.Identity,
                                        bias=sh[:, src_tile + t:src_tile + t + 1],
                                        scale=r[:, src_tile + t:src_tile + t + 1])
                last.then_inc(done, 1)

            def norm1_batch(b):
                wait(act, proj_ready, 8 * (b - 1) + 2 if b else 0)
                act.wait_ge(shift1_done, b)
                norm(b, b * TB, rstd, shift, xn, norm1)

            def load_function(function):
                col = warm_uses[0]
                warm_uses[0] += 1
                a.activation(warm[:, col:col + 1], mv[:, 0, 0:1], function)

            warm_uses = [0]

            def shared_gelu(i):
                for c in range(FC):
                    n = FC * i + c
                    act.wait_ge(sh.up, n + 1)
                    if i == SH_BEFORE and c == 0:
                        act.wait_ge(ex.h_lo, FC * SLOT_TILES)
                        act.wait_ge(ex.down, FC * SLOT_TILES)
                    if i != SH_ROOMY:
                        wait(act, sh.h_lo, sh_chunk_before(i, c))
                    if c == 0 and i < SH_ROOMY:
                        act.wait_ge(raw_lo, WEIGHT_PIECES)
                        wait(act, sh.tout, i)
                    bias = sb1_sb[:, c:c + 1]
                    last = a.activation(sh_hidden(i, c), sh_bank(i, c)[:, :], ACT.Gelu_apprx_tanh, bias=bias)
                    if i < SH_ROOMY or c in ACT_HIGH:
                        wait(act, sh.down, n - FC + 1)
                        last = a.activation(h_hi[:, c, :], sh_bank(i, c)[:, :], ACT.Gelu_apprx_tanh, bias=bias)
                    last.then_inc(sh.gelu, 1)

            def shared_out(i):
                act.wait_ge(sh.down, FC * (i + 1))
                wait(act, sh.tout, i - 1)
                if i == SH_BEFORE:
                    act.wait_ge(ex.tout, SLOT_TILES)
                a.activation(sh_yt(i), sh_out(i)[:, :], ACT.Identity, bias=sb2_sb[:, 0:1]).then_inc(sh.yt, 1)

            act.wait_ge(comb_ready, 1)
            a.activation(wcomb[:, :], bank[0][:, 0:3 * D], ACT.Copy).then_inc(comb_w, 1)

            def evacuate(b, j):
                act.wait_ge(proj_ready, 8 * b + j + 1)
                which = j // 2
                dst = (xnt, q_sb, k_sb[:, 1:], v_sb[b % 2][:, 1:])[which][:, (j % 2) * 512:(j % 2 + 1) * 512]
                if which == 0:
                    a.activation(dst, bank[j % 2][:, :], ACT.Copy).then_inc(proj_out, 1)
                else:
                    a.activation(dst, bank[j % 2][:, :], ACT.Identity, bias=bcomb[:, which - 1:which],
                                 scale=SCALE if which == 1 else 1.0).then_inc(proj_out, 1)

            def halo(b, buf, uses, done):
                act.wait_ge(proj_out, 8 * b + uses)
                a.activation(buf[:, 0:1], buf[:, SEQ:SEQ + 1], ACT.Copy)
                a.activation(buf[:, SEQ + 1:SEQ + 2], buf[:, 1:2], ACT.Copy).then_inc(done, 1)

            def exp_scores(c):
                act.wait_ge(shifted, c + 1)
                a.activation(soft[:, :, :], soft[:, :, :], ACT.Exp).then_inc(exps, 1)

            for b in range(BATCHES):
                wait(act, y_ready, 2 * (b - 1))
                evacuate(b, 0)
                evacuate(b, 1)
                wait(act, prod_done, b)
                if b == 0:
                    act.wait_ge(comb_b, 1)
                evacuate(b, 2)
                evacuate(b, 3)
                if b >= 1:
                    exp_scores(b - 1)
                evacuate(b, 4)
                evacuate(b, 5)
                halo(b, k_sb, 6, halo_k)
                probs_high(act, a, b - 1)
                wait(act, weighted_v, GROUPS * (b - 1))
                evacuate(b, 6)
                evacuate(b, 7)
                halo(b, v_sb[b % 2], 8, halo_v)
                transposed2(act, a, b - 2)
                if b == 2:
                    act.wait_ge(bias_in, 16 * 3)
                if b == BATCHES - 1:
                    load_function(ACT.Gelu_apprx_tanh)
                for i in shared_tiles(b)[:1]:
                    shared_gelu(i)
                if b + 1 < BATCHES:
                    norm1_batch(b + 1)
                for i in shared_tiles(b)[:1]:
                    shared_out(i)
                for i in shared_tiles(b)[1:]:
                    shared_gelu(i)
                if b == BATCHES - 1:
                    load_function(ACT.Exp)
            transposed2(act, a, BATCHES - 2)
            exp_scores(BATCHES - 1)
            probs_high(act, a, BATCHES - 1)
            shared_out(SH_FIRST_LEFT - 1)
            load_function(ACT.Gelu_apprx_tanh)
            shared_gelu(SH_FIRST_LEFT)
            transposed2(act, a, BATCHES - 1)
            shared_out(SH_FIRST_LEFT)
            shared_gelu(SH_FIRST_LEFT + 1)
            for i in range(SH_FIRST_LEFT + 2, SH_BEFORE):
                shared_gelu(i)
                shared_out(i - 1)
            shared_out(SH_BEFORE - 1)

            def slot_act(act, i, par, half):
                ph, tiles = ex, SLOT_TILES
                if runs(i, -1, tiles):
                    k = i + 1
                    act.wait_ge(ph.tin, k + 1)
                    wait(act, ph.up, FC * (k - 1))
                    a.activation(xs_hi[1 - par], bank[TIN][:, :], ACT.Copy).then_inc(ph.xs_hi, 1)
                def back():
                    k = i - 2
                    act.wait_ge(ph.tout, k + 1)
                    wait(act, ph.y_out[par], (half - 1) * 16 * SJ)
                    a.activation(y_sb[par], bank[TOUT][:, :].rearrange("p (j d) -> p j d", j=SJ), ACT.Copy)\
                        .then_inc(ph.y, 1)

                last_up = isinstance(i, int) and i == tiles - 1
                if last_up:
                    back()
                if runs(i, 0, tiles):
                    for c in range(FC):
                        act.wait_ge(ph.up, FC * i + c + 1)
                        wait(act, ph.h_lo, FC * (i - 1) + c + 1)
                        if c in ACT_HIGH:
                            wait(act, ph.down, FC * (i - 1) + c + 1)
                        bias = b_tile[:, bass.ds(i, 1), c:c + 1].rearrange("p a b -> p (a b)")
                        last = a.activation(h_sb[:, c, :], bank[c][:, :], ACT.Gelu_apprx_tanh, bias=bias)
                        if c in ACT_HIGH:
                            last = a.activation(h_hi[:, c, :], bank[c][:, :], ACT.Gelu_apprx_tanh, bias=bias)
                        last.then_inc(ph.gelu, 1)
                if runs(i, 2, tiles) and not last_up:
                    back()
                if runs(i, 1, tiles):
                    k = i - 1
                    act.wait_ge(ph.down, FC * i)
                    wait(act, ph.tout, k - 1)
                    a.activation(yt[1 - par], bank[DOWN][:, :], ACT.Identity,
                                 bias=b_tile[:, bass.ds(k, 1), FC:FC + 1].rearrange("p a b -> p (a b)"))\
                        .then_inc(ph.yt, 1)

            act.wait_ge(gap_ready, BATCHES)
            a.activation(gap[:, :], gap[:, :], ACT.Exp).then_inc(gap_exp, 1)
            load_function(ACT.Gelu_apprx_tanh)

            slot_act(act, -1, 1, -1)
            act.wait_ge(biases, 1)
            pipeline(act, SLOT_TILES, 1, 2, slot_act, done=1)

            for i in range(SH_BEFORE, SH_BEFORE + SH_BATCH):
                shared_gelu(i)
            for i in range(SH_BEFORE, SH_BEFORE + SH_BATCH):
                shared_out(i)

            act.wait_ge(gates, 1)
            for g in Y_ORDER:
                act.wait_ge(y_in[g], 16)
                for t in range(4):
                    first = y_back[g][:, t, D:2 * D]
                    last = a.activation(first, first, ACT.Copy, scale=gate1[:, g * 4 + t:g * 4 + t + 1])
                last.then_inc(scaled, 1)

        @block.vector
        def _(dve):
            v = nc.vector
            link = chain(dve, dve_step)

            def stats1_batch(b):
                dve.wait_ge(x_in[b], 16)
                for t in range(TB):
                    last = v.bn_stats(st[:, t, :], x_all[:, b * TB + t, :])
                link(last)
                for t in range(TB):
                    last = v.bn_aggr(mv[:, b * TB + t, :], st[:, t, :])
                last.then_inc(stat1, 1)
                dve.wait_ge(stat1, b + 1)

            def shift1(b):
                cols = slice(b * TB, (b + 1) * TB)
                dve.wait_ge(pow1, b + 1)
                v.scalar_tensor_tensor(shift[:, cols], mv[:, cols, 0], -1.0, rstd[:, cols], ALU.mult, ALU.mult)\
                    .then_inc(shift1_done, 1)

            stats1_batch(0)
            dve.wait_ge(pow1, 1)
            for t in range(TB):
                last = v.tensor_scalar(xn[:, t, :], x_all[:, t, :], mv[:, t, 0:1], rstd[:, t:t + 1],
                                       ALU.subtract, ALU.mult)
            last.then_inc(norm1, 1)
            dve.wait_ge(comb_ready, 1)
            link(v.tensor_tensor(bcomb[:, :], bank[1][:, 0:3], bqkv_sb, ALU.add))
            v.tensor_scalar(bcomb[:, 0:1], bcomb[:, 0:1], SCALE, None, ALU.mult).then_inc(comb_b, 1)
            link(v.tensor_copy(rw_parts[:, 0, :], rw_sb))
            v.tensor_tensor(rw_parts[:, 1, :], rw_sb, rw_parts[:, 0, :].bitcast(fp32), ALU.subtract)\
                .then_inc(rw_split, 1)
            for b in range(1, BATCHES):
                stats1_batch(b)
            dve.wait_ge(const_ready, 1)

            def softmax_shift(c):
                dve.wait_ge(scores, c + 1)
                wait(dve, probs_lo, c)
                s = scores_at.rearrange("p (n t) -> p n t", n=NEIGH)
                link(v.tensor_reduce(top[:, :], s.rearrange("p n t -> p t n"), X, ALU.max))
                v.tensor_tensor(soft[:, :, :], s, top[:, :].unsqueeze(1).to_broadcast([P, NEIGH, GT]),
                                ALU.subtract).then_inc(shifted, 1)

            def softmax(c):
                dve.wait_ge(exps, c + 1)
                link(v.tensor_reduce(inv[:, :], soft[:, :, :].rearrange("p n t -> p t n"), X, ALU.add))
                link(v.reciprocal(inv[:, :], inv[:, :]))
                v.tensor_tensor(soft[:, :, :], soft[:, :, :], inv[:, :].unsqueeze(1).to_broadcast([P, NEIGH, GT]),
                                ALU.mult).then_inc(probs, 1)
                dve.wait_ge(probs_hi, c + 1)
                v.tensor_tensor(p_lo[:, :, :], soft[:, :, :], p_hi[:, :, :].bitcast(fp32), ALU.subtract)\
                    .then_inc(probs_lo, 1)

            def products(b):
                dve.wait_ge(proj_out, 8 * b + 6)
                dve.wait_ge(halo_k, b + 1)
                wait(dve, scores, b)
                v.tensor_tensor(prod, q_sb.unsqueeze(1).to_broadcast([P, NEIGH, SEQ]), neighbours_of(k_sb, 0, SEQ),
                                ALU.mult).then_inc(prod_done, 1)

            def weigh(c, half):
                dve.wait_ge(halo_v, c + 1)
                for k in range(HALF_GROUPS):
                    use = GROUPS * c + HALF_GROUPS * half + k
                    dve.wait_ge(spread, use + 1)
                    if c < BATCHES - 1 or half == 0:
                        wait(dve, y_ready, 2 * c + half)
                    v.tensor_tensor(weighted_at(c, half)[:, :, k * GT:(k + 1) * GT],
                                    spread_at(use)[:, 0:NEIGH * GT].rearrange("p (n t) -> p n t", n=NEIGH),
                                    neighbours_of(v_sb[c % 2], (HALF_GROUPS * half + k) * GT, GT), ALU.mult)\
                        .then_inc(weighted_v, 1)

            def residual(c, j):
                dve.wait_ge(bo_added, c + 1)
                dve.wait_ge(y_ready, 2 * c + j + 1)
                part = x_all[:, c * TB + 4 * j:c * TB + 4 * j + 4, :]
                v.tensor_tensor(part, bank[5 + j][:, :].rearrange("p (t d) -> p t d", d=D), part, ALU.add)\
                    .then_inc(resid, 1)
                dve.wait_ge(resid, 2 * c + j + 1)
                for t in range(4 * j, 4 * j + 4):
                    last = v.bn_stats(st2[:, t, :], x_all[:, c * TB + t, :])
                if j == 1:
                    link(last)
                    for t in range(TB):
                        last = v.bn_aggr(mv2[:, t, :], st2[:, t, :])
                    link(last)

            def norm2_batch(c):
                v.tensor_scalar(neg_half[:, :], mv2[:, :, 1], EPS, -0.5, ALU.add, ALU.mult)
                link(v.tensor_scalar(rstd2[:, :], mv2[:, :, 1], EPS, None, ALU.add))
                link(v.tensor_single_scalar(guess[:, :], rstd2[:, :].bitcast(int32), 1, ALU.arith_shift_right))
                link(v.tensor_scalar(rstd2[:, :].bitcast(int32), guess[:, :], -1.0, float(0x5f3759df),
                                     ALU.mult, ALU.add))
                for _ in range(3):
                    link(v.tensor_tensor(square[:, :], rstd2[:, :], rstd2[:, :], ALU.mult))
                    link(v.tensor_tensor(square[:, :], square[:, :], neg_half[:, :], ALU.mult))
                    link(v.scalar_tensor_tensor(rstd2[:, :], square[:, :], 1.5, rstd2[:, :], ALU.add, ALU.mult))
                if c >= 2:
                    dve.wait_ge(scattered[c - 2], 16 * 2 * TB)
                    dve.wait_ge(t2_ready, 2 * (c - 1))
                for t in range(TB):
                    last = v.tensor_scalar(rows[c % 2][:, t, 0:D], x_all[:, c * TB + t, :], mv2[:, t, 0:1],
                                           rstd2[:, t:t + 1], ALU.subtract, ALU.mult)
                last.then_inc(norm2, 1)
                dve.wait_ge(norm2, c + 1)

            def transposed2(c):
                for j in range(2):
                    dve.wait_ge(xt_hi_done, 2 * c + j + 1)
                    cols = slice(c * SEQ + j * 512, c * SEQ + (j + 1) * 512)
                    v.tensor_tensor(xt_lo[:, cols], bank[5 + j][:, :], xt_hi[:, cols].bitcast(fp32), ALU.subtract)\
                        .then_inc(xt_lo_done, 1)

            over = lambda m: m[:, :].unsqueeze(2).to_broadcast([P, TB, EXPERTS])
            by_expert = lambda m: m[:, :].unsqueeze(1).to_broadcast([P, TB, EXPERTS])

            def choose(c):
                dve.wait_ge(logits, c + 1)
                link(v.tensor_tensor(lg[:, :, :], logits_at[:, :, 0, :], by_expert(rb_bc), ALU.add))
                link(v.tensor_tensor(lg[:, :, :], logits_at[:, :, 1, :], lg[:, :, :], ALU.add))
                for best, sel in ((m1, sel1), (m2, sel2)):
                    link(v.tensor_reduce(best[:, :], lg[:, :, :], X, ALU.max))
                    link(v.tensor_tensor(cand[:, :, :], lg[:, :, :], over(best), ALU.is_ge))
                    link(v.tensor_tensor(cand[:, :, :], cand[:, :, :], by_expert(rank_weight), ALU.mult))
                    link(v.tensor_reduce(km[:, :], cand[:, :, :], X, ALU.max))
                    link(v.tensor_tensor(sel[:, :, :], cand[:, :, :], over(km), ALU.is_equal))
                    if sel is sel1:
                        if c >= 2:
                            dve.wait_ge(scattered[c - 2], 16 * 2 * TB)
                        v.tensor_scalar(rows[c % 2][:, :, D + 1], km[:, :], -1.0, float(EXPERTS), ALU.mult, ALU.add)
                        link(v.scalar_tensor_tensor(lg[:, :, :], sel1[:, :, :], -3.0e38, lg[:, :, :],
                                                    ALU.mult, ALU.add))
                v.tensor_tensor(either[:, :, :], sel1[:, :, :], sel2[:, :, :], ALU.add).then_inc(chosen, 1)
                v.tensor_tensor(gap[:, c * TB:(c + 1) * TB], m2[:, :], m1[:, :], ALU.subtract).then_inc(gap_ready, 1)

            def place(c):
                tiles = slice(c * TB, (c + 1) * TB)
                dve.wait_ge(ranks, c + 1)
                link(v.tensor_tensor(slot_at[:, :, :], ranks_at, by_expert(base), ALU.add))
                v.tensor_tensor(base[:, :], counts_at, base[:, :], ALU.add)
                v.tensor_tensor(sel1[:, :, :], sel1[:, :, :], slot_at[:, :, :], ALU.mult)
                link(v.tensor_tensor(sel2[:, :, :], sel2[:, :, :], slot_at[:, :, :], ALU.mult))
                with nc.allow_low_precision(reason="row numbers are small integers"):
                    v.tensor_reduce(pos1[:, tiles], sel1[:, :, :], X, ALU.add)
                    v.tensor_reduce(pos2[:, tiles], sel2[:, :, :], X, ALU.add).then_inc(routed, 1)
                dve.wait_ge(routed, c + 1)

            def shared_split(i, chunks=range(FC)):
                for c in chunks:
                    n = FC * i + c
                    dve.wait_ge(sh.gelu, n + 1)
                    wait(dve, sh.down, n - FC + 1)
                    if i >= SH_ROOMY and c not in ACT_HIGH:
                        v.tensor_copy(h_hi[:, c, :], sh_hidden(i, c)).then_inc(sh.h_hi, 1)
                        dve.wait_ge(sh.h_hi, (FC - len(ACT_HIGH)) * (i - SH_ROOMY) + c // 2 + 1)
                    v.tensor_tensor(h_lo[:, c, :], sh_hidden(i, c), h_hi[:, c, :].bitcast(fp32),
                                    ALU.subtract).then_inc(sh.h_lo, 1)

            def shared_add(i):
                dve.wait_ge(sh.tout, i + 1)
                part = x_all[:, sh_at(i) * SJ:(sh_at(i) + 1) * SJ, :]
                v.tensor_tensor(part, sh_out(i)[:, :].rearrange("p (j d) -> p j d", j=SJ), part,
                                ALU.add).then_inc(sh.y, 1)

            def expert_ends():
                v.tensor_copy(pad_at[:, :], base[:, :]).then_inc(ends_known, 1)

            full = [P, SLOT_TILES, EXPERTS]

            def slot_tables():
                link(v.tensor_tensor(n_tiles[:, :], base[:, :], region_start[:, :], ALU.subtract))
                link(v.tensor_scalar(n_int[:, :], n_tiles[:, :], float(SLOT - 1), None, ALU.add))
                link(v.tensor_single_scalar(n_int[:, :], n_int[:, :], SLOT.bit_length() - 1, ALU.arith_shift_right))
                link(v.tensor_copy(n_tiles[:, :], n_int[:, :]))
                link(v.tensor_copy(ends[:, 0, 4:], n_int[:, :]))
                for k in range(3):
                    link(v.tensor_tensor(ends[:, k + 1, 4:], ends[:, k, 4:],
                                         ends[:, k, 4 - (1 << k):4 + EXPERTS - (1 << k)], ALU.add))
                link(v.tensor_tensor(passed, slot_no[:, :].unsqueeze(2).to_broadcast(full),
                                     ends[:, 3, 4:].unsqueeze(1).to_broadcast(full), ALU.is_ge))
                link(v.tensor_reduce(slot_expert[:, :], passed, X, ALU.add))
                link(v.tensor_tensor(passed_n, passed, n_tiles[:, :].unsqueeze(1).to_broadcast(full), ALU.mult))
                link(v.tensor_reduce(n_passed[:, :], passed_n, X, ALU.add))
                link(v.tensor_tensor(n_passed[:, :], slot_no[:, :], n_passed[:, :], ALU.subtract))
                link(v.tensor_scalar(row_of[:, :], slot_expert[:, :], float(REGION), None, ALU.mult))
                link(v.scalar_tensor_tensor(row_f[:, :], n_passed[:, :], float(SLOT), row_of[:, :],
                                            ALU.mult, ALU.add))
                link(v.tensor_scalar(slot_row[:, :], row_f[:, :], float(PAD_ROW), None, ALU.min))
                v.tensor_scalar(slot_w[:, :], slot_expert[:, :], float(EXPERTS - 1), None, ALU.min)\
                    .then_inc(tables, 1)

            def slot_biases():
                dve.wait_ge(bias_in, 16 * 3)
                link(v.tensor_tensor(passed, region_start[:, :].unsqueeze(1).to_broadcast(full),
                                     row_of[:, :].unsqueeze(2).to_broadcast(full), ALU.is_equal))
                each = [P, SLOT_TILES, FC + 1, EXPERTS]
                link(v.tensor_tensor(b_of, passed.unsqueeze(2).to_broadcast(each),
                                     b_all[:, :, :].rearrange("p e f -> p f e").unsqueeze(1).to_broadcast(each),
                                     ALU.mult))
                v.tensor_reduce(b_tile[:, :, :], b_of, X, ALU.add).then_inc(biases, 1)

            shift1(1)

            def split_weights(n):
                _, hi, lo = raw_piece(n)
                dve.wait_ge(raw_in[n % 2], 16 * (n // 2 + 1))
                v.tensor_copy(hi, raw[n % 2][:, :]).then_inc(raw_hi, 1)
                dve.wait_ge(raw_hi, n + 1)
                v.tensor_tensor(lo, raw[n % 2][:, :], hi.bitcast(fp32), ALU.subtract).then_inc(raw_lo, 1)

            for b in range(BATCHES):
                if b >= 1:
                    softmax_shift(b - 1)
                if b >= 1:
                    softmax(b - 1)
                if b < POOL_PRODUCTS:
                    products(b)
                if b == 0:
                    for later in range(2, BATCHES):
                        shift1(later)
                    for n in range(DVE_PIECES):
                        split_weights(n)
                if b >= 2:
                    transposed2(b - 2)
                if b >= 1:
                    weigh(b - 1, 0)
                if b >= 2:
                    choose(b - 2)
                for i in shared_tiles(b)[:1]:
                    shared_split(i)
                if b >= 1:
                    weigh(b - 1, 1)
                if b >= 2:
                    place(b - 2)
                if b >= 1:
                    residual(b - 1, 0)
                    residual(b - 1, 1)
                for i in shared_tiles(b)[1:]:
                    shared_split(i, (0, 1))
                if b >= 1:
                    norm2_batch(b - 1)
                for i in shared_tiles(b)[:1]:
                    shared_add(i)
            b = BATCHES - 1
            softmax_shift(b)
            transposed2(b - 1)
            shared_split(SH_FIRST_LEFT - 1, (2, 3))
            softmax(b)
            weigh(b, 0)
            weigh(b, 1)
            choose(b - 1)
            residual(b, 0)
            place(b - 1)
            residual(b, 1)
            norm2_batch(b)
            shared_add(SH_FIRST_LEFT - 1)
            shared_split(SH_FIRST_LEFT, (0, 1))
            transposed2(b)
            shared_split(SH_FIRST_LEFT, (2, 3))
            choose(b)
            shared_add(SH_FIRST_LEFT)
            place(b)
            expert_ends()
            shared_split(SH_FIRST_LEFT + 1)
            shared_split(SH_FIRST_LEFT + 2)
            shared_add(SH_FIRST_LEFT + 1)
            slot_tables()
            shared_split(SH_BEFORE - 1)
            shared_add(SH_BEFORE - 2)
            slot_biases()
            shared_add(SH_BEFORE - 1)

            dve.wait_ge(gap_exp, 1)
            link(v.tensor_scalar(gate2[:, :], gap[:, :], 1.0, None, ALU.add))
            link(v.reciprocal(gate1[:, :], gate2[:, :]))
            v.tensor_tensor(gate2[:, :], gate1[:, :], gap[:, :], ALU.mult).then_inc(gates, 1)

            def slot_dve(dve, i, par, half):
                ph, tiles = ex, SLOT_TILES
                if runs(i, -1, tiles):
                    k, kpar = i + 1, 1 - par
                    dve.wait_ge(ph.rows_in[kpar], (half + par + 1) * 16)
                    v.scalar_tensor_tensor(y_rows[:, bass.ds(k * SJ, SJ)], xs[kpar][:, :, D + 1],
                                           slot_expert[:, bass.ds(k, 1)], xs[kpar][:, :, D],
                                           ALU.is_equal, ALU.add).then_inc(ph.idx, 1)
                    dve.wait_ge(ph.xs_hi, k + 1)
                    v.tensor_tensor(xs_lo[kpar], bank[TIN][:, :], xs_hi[kpar].bitcast(fp32),
                                    ALU.subtract).then_inc(ph.xs_lo, 1)
                if runs(i, 0, tiles):
                    for c in range(FC):
                        dve.wait_ge(ph.gelu, FC * i + c + 1)
                        wait(dve, ph.down, FC * (i - 1) + c + 1)
                        if c not in ACT_HIGH:
                            v.tensor_copy(h_hi[:, c, :], h_sb[:, c, :]).then_inc(ph.h_hi, 1)
                            dve.wait_ge(ph.h_hi, (FC - len(ACT_HIGH)) * i + c // 2 + 1)
                        v.tensor_tensor(h_lo[:, c, :], h_sb[:, c, :], h_hi[:, c, :].bitcast(fp32),
                                        ALU.subtract).then_inc(ph.h_lo, 1)
            pipeline(dve, SLOT_TILES, 1, 2, slot_dve)

            for i in range(SH_BEFORE, SH_BEFORE + SH_BATCH):
                shared_split(i)
            for i in range(SH_BEFORE, SH_BEFORE + SH_BATCH):
                shared_add(i)
            dve.wait_ge(sh.y, SH_BEFORE + SH_BATCH)
            dve.wait_ge(gates, 1)

            for g in Y_ORDER:
                dve.wait_ge(y_in[g], 16)
                for t in range(4):
                    tile = g * 4 + t
                    ins = v.scalar_tensor_tensor(x_all[:, tile, :], y_back[g][:, t, 0:D], gate2[:, tile:tile + 1],
                                                 x_all[:, tile, :], ALU.mult, ALU.add)
                ins.then_inc(second_in, 1)

        @block.tensor
        def _(pe):
            m = nc.tensor
            pe.wait_ge(w_in, W_LOADS)
            m.matmul(bank[0][:, 0:3 * D], wp_sb, wqkv_sb, start=True, stop=True)
            for i in range(3):
                last = m.matmul(bank[1][:, i:i + 1], wqkv_sb[:, i * D:(i + 1) * D], bp_sb, start=True, stop=True)
            last.then_inc(comb_ready, 1)

            def project(b, uses):
                for j in uses:
                    use = 8 * b + j
                    wait(pe, proj_out, use - 1)
                    to = bank[use % 2]
                    if j < 2:
                        if b == 0:
                            pe.wait_ge(comb_w if j == 0 else comb_b, 1)
                        pe.wait_ge(norm1, b + 1)
                        for t in range(4):
                            last = m.transpose(to[:, t * D:(t + 1) * D], xn[:, 4 * j + t, :], ident[:, :])
                    else:
                        if j == 2:
                            pe.wait_ge(comb_w, 1)
                            pe.wait_ge(proj_out, 8 * b + 2)
                        w = (j - 2) // 2
                        last = m.matmul(to[:, :], wcomb[:, w * D:(w + 1) * D], xnt[:, (j % 2) * 512:(j % 2 + 1) * 512],
                                        start=True, stop=True)
                    last.then_inc(proj_ready, 1)

            def score(b):
                pe.wait_ge(prod_done, b + 1)
                wait(pe, shifted, b)
                wait(pe, routed, b - 1)
                for grp in range(GROUPS):
                    off = P - HEADS - HEADS * grp
                    last = m.matmul(scores_at, score_mask[:, off:off + P], prod[:, :, grp * GT:(grp + 1) * GT],
                                    start=(grp == 0), stop=(grp == GROUPS - 1))
                last.then_inc(scores, 1)

            def spread_probs(c, half, groups=range(HALF_GROUPS)):
                pe.wait_ge(probs_lo, c + 1)
                for k in groups:
                    use = GROUPS * c + HALF_GROUPS * half + k
                    wait(pe, weighted_v, use - 1 if use < LAST else max(LAST, use - 3))
                    to = spread_at(use)[:, 0:NEIGH * GT]
                    mask = expand[:, HALF_GROUPS * half + k, :]
                    m.matmul(to, mask, p_hi[:, :, :], start=True, stop=False)
                    m.matmul(to, mask, p_lo[:, :, :], start=False, stop=True).then_inc(spread, 1)

            def out_project(c, half):
                pe.wait_ge(weighted_v, (2 * c + half + 1) * HALF_GROUPS)
                wait(pe, xt_lo_done, 2 * (c - 1) + half + 1 if c else 0)
                for t in range(4):
                    for n in range(NEIGH):
                        last = m.matmul(bank[5 + half][:, t * D:(t + 1) * D],
                                        weighted_at(c, half)[:, n, t * P:(t + 1) * P], wo_sb,
                                        start=(n == 0), stop=(n == NEIGH - 1))
                last.then_inc(y_ready, 1)

            def transpose2(c):
                pe.wait_ge(norm2, c + 1)
                pe.wait_ge(resid, 2 * (c + 1))
                for j in range(2):
                    for t in range(4):
                        last = m.transpose(bank[5 + j][:, t * D:(t + 1) * D], rows[c % 2][:, 4 * j + t, 0:D],
                                           ident[:, :])
                    last.then_inc(t2_ready, 1)

            def router(c):
                pe.wait_ge(xt_lo_done, 2 * (c + 1))
                pe.wait_ge(rw_split, 1)
                wait(pe, routed, c)
                for t in range(TB):
                    cols = slice((c * TB + t) * P, (c * TB + t + 1) * P)
                    to = logits_at[:, t, :, :]
                    m.matmul(to[:, :, :], xt_hi[:, cols], rw_parts[:, :, :], start=True, stop=False)
                    last = m.matmul(to[:, 0, :], xt_lo[:, cols], rw_parts[:, 0, :], start=False, stop=True)
                last.then_inc(logits, 1)

            def rank(c):
                pe.wait_ge(chosen, c + 1)
                to = ranks_at
                m.matmul(to, before[:, :], either[:, :, :], start=True, stop=False, skip_group_check=True)
                for back in range(1, TB):
                    m.matmul(to[:, back:, :], ones_bf[:, :], either[:, 0:TB - back, :], start=False,
                             stop=(back == TB - 1), skip_group_check=True)
                for t in range(TB):
                    last = m.matmul(counts_at, ones_bf[:, :], either[:, t, :],
                                    start=(t == 0), stop=(t == TB - 1), skip_group_check=True)
                last.then_inc(ranks, 1)

            def shared_up(i, chunks=range(FC)):
                at = sh_at(i)
                pe.wait_ge(xt_lo_done, at + 1)
                if i == 0:
                    pe.wait_ge(raw_lo, 2)
                    pe.wait_ge(proj_out, 8 * BATCHES)
                if i == SH_BEFORE:
                    pe.wait_ge(ex.gelu, FC * SLOT_TILES)
                    pe.wait_ge(ex.xs_lo, SLOT_TILES)
                cols = slice(at * SLOT, (at + 1) * SLOT)
                for c in chunks:
                    wait(pe, sh.gelu, sh_chunk_before(i, c))
                    to, w = sh_bank(i, c)[:, :], sw[:, :, c * P:(c + 1) * P]
                    m.matmul(to, w[:, 0, :], xt_hi[:, cols], start=True, stop=False)
                    m.matmul(to, w[:, 0, :], xt_lo[:, cols], start=False, stop=False)
                    m.matmul(to, w[:, 1, :], xt_hi[:, cols], start=False, stop=True).then_inc(sh.up, 1)

            def shared_down(i, chunks=range(FC)):
                wait(pe, sh.y, i if i <= SH_ROOMY else i - 1)
                if i == SH_BEFORE + 1:
                    pe.wait_ge(ex.y, SLOT_TILES)
                for c in chunks:
                    pe.wait_ge(sh.h_lo, FC * i + c + 1)
                    to, w = sh_out(i)[:, :], sw[:, :, c * P:(c + 1) * P]
                    m.matmul(to, w[:, 2, :], h_hi[:, c, :], start=(c == 0), stop=False)
                    m.matmul(to, w[:, 2, :], h_lo[:, c, :], start=False, stop=False)
                    m.matmul(to, w[:, 3, :], h_hi[:, c, :], start=False, stop=(c == FC - 1)).then_inc(sh.down, 1)

            def shared_back(i):
                pe.wait_ge(sh.yt, i + 1)
                for j in range(SJ):
                    last = m.transpose(sh_out(i)[:, j * P:(j + 1) * P], sh_yt(i)[:, j * P:(j + 1) * P], ident[:, :])
                last.then_inc(sh.tout, 1)

            for b in range(BATCHES):
                project(b, range(8))
                if b >= 2:
                    transpose2(b - 2)
                if b >= 1:
                    spread_probs(b - 1, 0, (0, 1))
                if b >= 2:
                    router(b - 2)
                if b >= 1:
                    spread_probs(b - 1, 0, (2, 3))
                for i in shared_tiles(b)[:1]:
                    shared_up(i)
                if b >= 1:
                    out_project(b - 1, 0)
                if b >= 2:
                    rank(b - 2)
                if b >= 1:
                    spread_probs(b - 1, 1, (0, 1))
                for i in shared_tiles(b)[:1]:
                    shared_down(i)
                if b >= 1:
                    spread_probs(b - 1, 1, (2, 3))
                    out_project(b - 1, 1)
                for i in shared_tiles(b)[:1]:
                    shared_back(i)
                for i in shared_tiles(b)[1:]:
                    shared_up(i)
                score(b)
            b = BATCHES - 1
            transpose2(b - 1)
            router(b - 1)
            spread_probs(b, 0)
            spread_probs(b, 1)
            out_project(b, 0)
            rank(b - 1)
            out_project(b, 1)
            shared_down(SH_FIRST_LEFT - 1)
            shared_back(SH_FIRST_LEFT - 1)
            shared_up(SH_FIRST_LEFT)
            transpose2(b)
            shared_down(SH_FIRST_LEFT, (0, 1))
            router(b)
            shared_down(SH_FIRST_LEFT, (2, 3))
            shared_back(SH_FIRST_LEFT)
            rank(b)
            shared_up(SH_FIRST_LEFT + 1)
            shared_up(SH_FIRST_LEFT + 2)
            shared_down(SH_FIRST_LEFT + 1)
            shared_up(SH_BEFORE - 1)
            shared_back(SH_FIRST_LEFT + 1)
            shared_down(SH_BEFORE - 2)
            shared_back(SH_BEFORE - 2)
            shared_down(SH_BEFORE - 1)
            shared_back(SH_BEFORE - 1)

            def slot_pe(pe, i, par, half):
                ph, tiles = ex, SLOT_TILES
                if runs(i, -1, tiles):
                    k, kpar = i + 1, 1 - par
                    pe.wait_ge(ph.rows_in[kpar], (half + par + 1) * 16)
                    wait(pe, ph.xs_lo, k)
                    for j in range(SJ):
                        last = m.transpose(bank[TIN][:, j * P:(j + 1) * P], xs[kpar][:, j, 0:D], ident[:, :])
                    last.then_inc(ph.tin, 1)
                def back():
                    pe.wait_ge(ph.yt, i - 1)
                    wait(pe, ph.y, i - 2)
                    for j in range(SJ):
                        last = m.transpose(bank[TOUT][:, j * P:(j + 1) * P], yt[par][:, j * P:(j + 1) * P], ident[:, :])
                    last.then_inc(ph.tout, 1)

                last_up = isinstance(i, int) and i == tiles - 1
                if last_up:
                    back()
                if runs(i, 0, tiles):
                    w, hi, lo = stage[par], xs_hi[par], xs_lo[par]
                    pe.wait_ge(ph.w_in[0][par], (half + 1) * 16)
                    pe.wait_ge(ph.xs_lo, i + 1)
                    for c in range(FC):
                        wait(pe, ph.gelu, FC * (i - 1) + c + 1)
                        w_hi, w_lo = w[:, 0, c * P:(c + 1) * P], w[:, 1, c * P:(c + 1) * P]
                        m.matmul(bank[c][:, :], w_hi, hi, start=True, stop=False)
                        m.matmul(bank[c][:, :], w_hi, lo, start=False, stop=False)
                        m.matmul(bank[c][:, :], w_lo, hi, start=False, stop=True).then_inc(ph.up, 1)
                if runs(i, 2, tiles) and not last_up:
                    back()
                if runs(i, 1, tiles):
                    k = i - 1
                    w = stage[1 - par]
                    pe.wait_ge(ph.w_in[1][1 - par], (half + par) * 16)
                    wait(pe, ph.yt, k)
                    for c in range(FC):
                        pe.wait_ge(ph.h_lo, FC * k + c + 1)
                        w_hi, w_lo = w[:, 2, c * P:(c + 1) * P], w[:, 3, c * P:(c + 1) * P]
                        m.matmul(bank[DOWN][:, :], w_hi, h_hi[:, c, :], start=(c == 0), stop=False)
                        m.matmul(bank[DOWN][:, :], w_hi, h_lo[:, c, :], start=False, stop=False)
                        m.matmul(bank[DOWN][:, :], w_lo, h_hi[:, c, :], start=False, stop=(c == FC - 1))\
                            .then_inc(ph.down, 1)

            pipeline(pe, SLOT_TILES, 1, 2, slot_pe)

            for i in range(SH_BEFORE, SH_BEFORE + SH_BATCH):
                shared_up(i)
            for i in range(SH_BEFORE, SH_BEFORE + SH_BATCH):
                shared_down(i)
                shared_back(i)

    return nc


def kernel(**inputs):
    import numpy as np
    import concourse.bacc as bacc
    from concourse.bass_utils import run_bass_kernel_spmd

    p = {k.replace("L0_", ""): np.asarray(v) for k, v in inputs.items()}
    t = lambda a: np.ascontiguousarray(np.swapaxes(a, -1, -2))
    chunks = lambda a: np.ascontiguousarray(a.reshape(a.shape[:-1] + (-1, P)).swapaxes(-1, -2))
    arrays = {
        "x": p["attn_x"],
        "attn_w": np.concatenate([p["attn_Wp"], t(p["attn_Wq"]), t(p["attn_Wk"]), t(p["attn_Wv"]), t(p["attn_Wo"]),
                                  t(p["ffn_router_w"]), p["attn_bp"][:, None], p["attn_bq"][:, None],
                                  p["attn_bk"][:, None], p["attn_bv"][:, None]], axis=1),
        "bo": p["attn_bo"],
        "sw1_t": t(p["ffn_shared_w1"]),
        "sb1": chunks(p["ffn_shared_b1"]),
        "sw2_t": t(p["ffn_shared_w2"]),
        "sb2": p["ffn_shared_b2"],
        "rb": p["ffn_router_b"],
        "ew1_t": t(p["ffn_spec_w1"]),
        "ew2_t": t(p["ffn_spec_w2"]),
        "eb": np.concatenate([chunks(p["ffn_spec_b1"]).swapaxes(0, 1), t(p["ffn_spec_b2"])[:, :, None]], axis=2),
    }
    nc = bacc.Bacc("TRN2", target_bir_lowering=False, num_devices=1)
    args = {}
    for name, a in arrays.items():
        arrays[name] = a = np.ascontiguousarray(a)
        args[name] = nc.dram_tensor(name, a.shape, mybir.dt.from_np(a.dtype), kind="ExternalInput").ap()
    out = nc.dram_tensor("out", (BATCHES, SEQ, D), mybir.dt.float32, kind="ExternalOutput").ap()
    preln_local_attention_moe(nc, **args, out=out)
    r = run_bass_kernel_spmd(nc, [arrays], core_ids=[0])
    return r.results[0]["out"]
```
